# Optimizing a Trainium2 kernel written in Bass

```python
import numpy as np
import jax
import jax.numpy as jnp

def _softmax(x, axis=-1):
    return jax.nn.softmax(x, axis=axis)

def _gelu(x):
    return jax.nn.gelu(x, approximate=True)

def _silu(x):
    return jax.nn.silu(x)

def _sigmoid(x):
    return jax.nn.sigmoid(x)

def _layernorm(x, axis=-1, eps=1e-05):
    m = jnp.mean(x, axis=axis, keepdims=True)
    v = jnp.var(x, axis=axis, keepdims=True)
    return (x - m) / jnp.sqrt(v + eps)

def _scatter_add(tgt, idx, src, axis=0):
    return tgt.at[idx].add(src)

def _segment_sum(src, seg, n):
    return jax.ops.segment_sum(src, seg, n)
kernel_name = 'mk_decoder_preln_d1_seqx_r2_5d5f21'

def setup_inputs(seed: int=0):
    np.random.seed(seed)
    _w = jnp.asarray

    def _rec_inputs():
        import jax
        import jax.numpy as jnp
        _rk = jax.random.key(seed)
        x = -0.0003929 + 0.9999 * jax.random.normal(jax.random.fold_in(_rk, 1), (2, 1024, 512), jnp.float32)
        _lenS = 1024 - jax.random.randint(jax.random.fold_in(_rk, 7), (2,), 0, max(1, 1024 // 4) + 1, jnp.int32)
        _lenS2 = 2048 - jax.random.randint(jax.random.fold_in(_rk, 8), (2,), 0, max(1, 2048 // 4) + 1, jnp.int32)
        _ctx_1024P = jax.random.normal(jax.random.fold_in(_rk, 11), (2, 16, 512), jnp.float32)
        _ctx_1024c = jax.random.dirichlet(jax.random.fold_in(_rk, 511), 0.3 * jnp.ones((16,), jnp.float32), (2, 2048))
        _ctx_1024t = jnp.einsum('bsk,bkd->bsd', _ctx_1024c, _ctx_1024P)
        _ctx_1024t = _ctx_1024t * jax.lax.rsqrt(jnp.mean(jnp.square(_ctx_1024t)) + 1e-12) * 0.953939
        ctx_1024 = 2.81802e-05 + 1.00001 * (_ctx_1024t + 0.3 * jax.random.normal(jax.random.fold_in(_rk, 611), (2, 2048, 512), jnp.float32))
        return (x, ctx_1024)
    x, ctx_1024 = _rec_inputs()

    def _L0_attn_setup():
        import jax, jax.numpy as jnp
        import numpy as np
        D_MODEL = 512
        N_HEADS = 16
        D_HEAD = D_MODEL // N_HEADS
        K_WIN = 8
        DILATION = 2
        EPS = 1e-06

        def _dilated_mask(N):
            i = jnp.arange(N)[:, None]
            j = jnp.arange(N)[None, :]
            diff = j - i
            return (jnp.abs(diff) <= K_WIN * DILATION) & (jnp.mod(diff, DILATION) == 0)
        key = jax.random.key(seed)
        ks = jax.random.split(key, 5)
        B, N = (2, 1024)
        s_in = 1.0 / np.sqrt(D_MODEL)
        x = jax.random.normal(ks[0], (B, N, D_MODEL), dtype=jnp.float32)
        qkv_w = jax.random.uniform(ks[1], (3 * D_MODEL, D_MODEL), dtype=jnp.float32, minval=-s_in, maxval=s_in)
        qkv_b = jax.random.uniform(ks[2], (3 * D_MODEL,), dtype=jnp.float32, minval=-s_in, maxval=s_in)
        out_w = jax.random.uniform(ks[3], (D_MODEL, D_MODEL), dtype=jnp.float32, minval=-s_in, maxval=s_in)
        out_b = jax.random.uniform(ks[4], (D_MODEL,), dtype=jnp.float32, minval=-s_in, maxval=s_in)
        return {'x': x, 'qkv_w': qkv_w, 'qkv_b': qkv_b, 'out_w': out_w, 'out_b': out_b}
    _L0_attn_all = _L0_attn_setup()
    _L0_attn_in = {k: v for k, v in _L0_attn_all.items() if k in ('qkv_w', 'qkv_b', 'out_w', 'out_b')}
    del _L0_attn_all

    def _L0_xattn_setup():
        import jax, jax.numpy as jnp
        import numpy as np
        B, L, D = (8, 1024, 512)
        key = jax.random.key(seed)
        ks = jax.random.split(key, 9)
        scale = 1.0 / np.sqrt(D)
        return {'query_source': jax.random.normal(ks[0], (B, L, D), dtype=jnp.float32), 'key_source': jax.random.normal(ks[1], (B, L, D), dtype=jnp.float32), 'value_source': jax.random.normal(ks[2], (B, L, D), dtype=jnp.float32), 'Wq': jax.random.normal(ks[3], (D, D), dtype=jnp.float32) * scale, 'bq': jnp.zeros((D,), dtype=jnp.float32), 'Wk': jax.random.normal(ks[4], (D, D), dtype=jnp.float32) * scale, 'bk': jnp.zeros((D,), dtype=jnp.float32), 'Wv': jax.random.normal(ks[5], (D, D), dtype=jnp.float32) * scale, 'bv': jnp.zeros((D,), dtype=jnp.float32)}
    _L0_xattn_all = _L0_xattn_setup()
    _L0_xattn_in = {k: v for k, v in _L0_xattn_all.items() if k in ('Wq', 'bq', 'Wk', 'bk', 'Wv', 'bv')}
    del _L0_xattn_all

    def _L0_ffn_setup():
        import jax, jax.numpy as jnp
        import numpy as np
        DIM = 512
        HIDDEN = 1536
        SCALE = 1.0 / 127.0

        def _dequant(w_int, dtype):
            return w_int.astype(dtype) * jnp.asarray(SCALE, dtype)
        key = jax.random.key(seed)
        k_x, k_g, k_u, k_d = jax.random.split(key, 4)
        x = jax.random.normal(k_x, (4, 1024, DIM), dtype=jnp.float32)
        w_gate = jax.random.randint(k_g, (HIDDEN, DIM), -127, 128, dtype=jnp.int32)
        w_up = jax.random.randint(k_u, (HIDDEN, DIM), -127, 128, dtype=jnp.int32)
        w_down = jax.random.randint(k_d, (DIM, HIDDEN), -127, 128, dtype=jnp.int32)
        return {'x': x, 'w_gate': w_gate, 'w_up': w_up, 'w_down': w_down}
    _L0_ffn_all = _L0_ffn_setup()
    _L0_ffn_in = {k: v for k, v in _L0_ffn_all.items() if k in ('w_gate', 'w_up', 'w_down')}
    del _L0_ffn_all
    return {'x': x, 'ctx_1024': ctx_1024, 'L0_attn_qkv_w': _L0_attn_in['qkv_w'], 'L0_attn_qkv_b': _L0_attn_in['qkv_b'], 'L0_attn_out_w': _L0_attn_in['out_w'], 'L0_attn_out_b': _L0_attn_in['out_b'], 'L0_xattn_Wq': _L0_xattn_in['Wq'], 'L0_xattn_bq': _L0_xattn_in['bq'], 'L0_xattn_Wk': _L0_xattn_in['Wk'], 'L0_xattn_bk': _L0_xattn_in['bk'], 'L0_xattn_Wv': _L0_xattn_in['Wv'], 'L0_xattn_bv': _L0_xattn_in['bv'], 'L0_ffn_w_gate': _L0_ffn_in['w_gate'], 'L0_ffn_w_up': _L0_ffn_in['w_up'], 'L0_ffn_w_down': _L0_ffn_in['w_down']}

def reference(x, ctx_1024, L0_attn_qkv_w, L0_attn_qkv_b, L0_attn_out_w, L0_attn_out_b, L0_xattn_Wq, L0_xattn_bq, L0_xattn_Wk, L0_xattn_bk, L0_xattn_Wv, L0_xattn_bv, L0_ffn_w_gate, L0_ffn_w_up, L0_ffn_w_down):
    import jax
    import jax.numpy as jnp

    def _L0_attn_ref(x, qkv_w, qkv_b, out_w, out_b):
        import jax, jax.numpy as jnp
        import numpy as np
        D_MODEL = 512
        N_HEADS = 16
        D_HEAD = D_MODEL // N_HEADS
        K_WIN = 8
        DILATION = 2
        EPS = 1e-06

        def _dilated_mask(N):
            i = jnp.arange(N)[:, None]
            j = jnp.arange(N)[None, :]
            diff = j - i
            return (jnp.abs(diff) <= K_WIN * DILATION) & (jnp.mod(diff, DILATION) == 0)
        B, N, D = x.shape
        qkv = x @ qkv_w.T + qkv_b
        q, k, v = jnp.split(qkv, 3, axis=-1)

        def heads(t):
            return t.reshape(B, N, N_HEADS, D_HEAD).transpose(0, 2, 1, 3)
        q, k, v = (heads(q), heads(k), heads(v))
        q = q / (jnp.linalg.norm(q, axis=-1, keepdims=True) + EPS)
        k = k / (jnp.linalg.norm(k, axis=-1, keepdims=True) + EPS)
        scale = jnp.float32(1.0)
        allowed = _dilated_mask(N)
        scores = jnp.einsum('bhnd,bhmd->bhnm', q, k) * scale
        scores = jnp.where(allowed[None, None], scores, -jnp.inf)
        attn = jax.nn.softmax(scores, axis=-1)
        out = jnp.einsum('bhnm,bhmd->bhnd', attn, v)
        out = out.transpose(0, 2, 1, 3).reshape(B, N, D)
        return out @ out_w.T + out_b

    def _L0_xattn_ref(query_source, key_source, value_source, Wq, bq, Wk, bk, Wv, bv):
        import jax, jax.numpy as jnp
        import numpy as np
        B, L, D = (8, 1024, 512)
        q = query_source @ Wq + bq
        k = key_source @ Wk + bk
        v = value_source @ Wv + bv
        scores = jnp.einsum('bqd,bkd->bqk', q, k)
        attn = jax.nn.softmax(scores, axis=-1)
        out = jnp.einsum('bqk,bkd->bqd', attn, v)
        return out

    def _L0_ffn_ref(x, w_gate, w_up, w_down):
        import jax, jax.numpy as jnp
        import numpy as np
        DIM = 512
        HIDDEN = 1536
        SCALE = 1.0 / 127.0

        def _dequant(w_int, dtype):
            return w_int.astype(dtype) * jnp.asarray(SCALE, dtype)
        wg = _dequant(w_gate, x.dtype)
        wu = _dequant(w_up, x.dtype)
        wd = _dequant(w_down, x.dtype)
        gate = jnp.einsum('bsd,hd->bsh', x, wg)
        up = jnp.einsum('bsd,hd->bsh', x, wu)
        h = jax.nn.silu(gate) * up
        return jnp.einsum('bsh,dh->bsd', h, wd)
    x = x + _L0_attn_ref(_layernorm(x, axis=-1), L0_attn_qkv_w, L0_attn_qkv_b, L0_attn_out_w, L0_attn_out_b)
    x = x + _L0_xattn_ref(_layernorm(x, axis=-1), ctx_1024, ctx_1024, L0_xattn_Wq, L0_xattn_bq, L0_xattn_Wk, L0_xattn_bk, L0_xattn_Wv, L0_xattn_bv)
    x = x + _L0_ffn_ref(_layernorm(x, axis=-1), L0_ffn_w_gate, L0_ffn_w_up, L0_ffn_w_down)
    return x

_drawn_inputs = setup_inputs


def setup_inputs(seed=0):
    import zlib

    import numpy as np

    out = dict(_drawn_inputs(seed))
    spreads = {'L0_xattn_bq': (0.0, 0.1), 'L0_xattn_bk': (0.0, 0.1), 'L0_xattn_bv': (0.0, 0.1)}
    factors = {}
    for name, (base, spread) in spreads.items():
        noise = np.random.default_rng([zlib.crc32(name.encode()), seed]).standard_normal(out[name].shape)
        drawn = base * np.exp(spread * noise) if base else spread * noise
        out[name] = jnp.asarray(drawn.astype(out[name].dtype))
    for name, factor in factors.items():
        out[name] = (out[name] * factor).astype(out[name].dtype)
    return out
```

```python
from contextlib import ExitStack

import concourse.bass as bass
from concourse import mybir

F32 = mybir.dt.float32
F32R = mybir.dt.float32r
I32 = mybir.dt.int32
ALU = mybir.AluOpType
ACT = mybir.ActivationFunctionType
AX = mybir.AxisListType

P = 128
NB = 2
T = 2048
D = 512
DK = D // P
SEQ = 512
ST = SEQ // P
NT = T // P
HG = 4
HPG = 4
DH = 32
H = HG * HPG
HALO = 8
WIN = P + 2 * HALO
CTX = 2048
CK = CTX // P
BT = T // NB // P
FH = 1536
FK = FH // P
NBLK = T // SEQ
LN_EPS = 1e-5
NORM_EPS = 1e-6
WSCALE = 1.0 / 127.0


def three(pe, out, hi_s, lo_s, hi_m, lo_m, first, last):
    pe.matmul(out, hi_s, hi_m, start=first, stop=False)
    pe.matmul(out, hi_s, lo_m, start=False, stop=False)
    return pe.matmul(out, lo_s, hi_m, start=False, stop=last)


def decoder_layer(nc, x, ctx_n, ctx_t, wqkv_t, qkv_b, wo_t, out_b, wq_t, bq, wk_t, bk, wv, bv,
                  wg_t, wu_t, wd_t, out):
    x1_dram = nc.dram_tensor("x1_scratch", [T, D], F32, kind="Internal").ap()
    x2_dram = nc.dram_tensor("x2_scratch", [T, D], F32, kind="Internal").ap()
    qp_dram = nc.dram_tensor("qp_scratch", [NT, P, D], F32, kind="Internal").ap()
    with ExitStack() as ctx:
        def sb(scope, name, shape, dt=F32):
            return scope.enter_context(nc.sbuf_tensor(name, shape, dt))

        def sem(name):
            return ctx.enter_context(nc.semaphore(name))

        score = ctx.enter_context(nc.psum_tensor("score", [P, 4, 512], F32))
        work = ctx.enter_context(nc.psum_tensor("work", [P, 4, 512], F32))
        wait_pad = sb(ctx, "wait_pad", [P, 1 + ST])
        ident = sb(ctx, "ident", [P, P])
        mhalf = sb(ctx, "mhalf", [P, 2 * H])
        half = sb(ctx, "half", [P, 2 * H])
        q_const = sb(ctx, "q_const", [P, NT])

        with ExitStack() as attn:
            attention_phase(nc, ctx, attn, sb, sem, score, work, ident, mhalf, wait_pad, half, q_const,
                            x, wqkv_t, qkv_b, wo_t, out_b, wq_t, bq, wk_t, bk, x1_dram, qp_dram)
        with ExitStack() as cross:
            cross_phase(nc, cross, sb, sem, score, work, ident, q_const,
                        ctx_n, ctx_t, wv, bv, x1_dram, qp_dram, x2_dram)
        with ExitStack() as ffn:
            ffn_phase(nc, ffn, sb, sem, score, work, ident, mhalf, wait_pad, wg_t, wu_t, wd_t, x2_dram, out)


def attention_phase(nc, ctx, scope, sb, sem, score, work, ident, mhalf, wait_pad, half, q_const,
                    x, wqkv_t, qkv_b, wo_t, out_b, wq_t, bq, wk_t, bk, x1_dram, qp_dram):
    wqkv_h = sb(scope, "wqkv_h", [P, DK, 3 * D], F32R)
    wqkv_l = sb(scope, "wqkv_l", [P, DK, 3 * D], F32R)
    wo_h = sb(scope, "wo_h", [P, DK, D], F32R)
    wo_l = sb(scope, "wo_l", [P, DK, D], F32R)
    wp_h = sb(scope, "wp_h", [P, DK, D], F32R)
    wp_l = sb(scope, "wp_l", [P, DK, D], F32R)
    qkvb_row = sb(scope, "qkvb_row", [P, 3 * D])
    ob_row = sb(scope, "ob_row", [P, D])
    wqb_row = sb(scope, "wqb_row", [P, D])
    bqp = sb(scope, "bqp", [P, DK])
    bqbk = sb(scope, "bqbk", [P, 1])
    ones = sb(scope, "ones", [P, DH])
    band = sb(scope, "band", [P, WIN])

    with ExitStack() as st:
        raw = sb(st, "w_raw", [P, DK, 3 * D])
        raw_o = sb(st, "wo_raw", [P, DK, D])
        raw_q = sb(st, "wq_raw", [P, DK, D])
        raw_k = sb(st, "wk_raw", [P, DK, D])
        q_h = sb(st, "wq_h", [P, DK, D], F32R)
        q_l = sb(st, "wq_l", [P, DK, D], F32R)
        k_h = sb(st, "wk_h", [P, DK, D], F32R)
        k_l = sb(st, "wk_l", [P, DK, D], F32R)
        bq_col = sb(st, "bq_col", [P, DK])
        bk_col = sb(st, "bk_col", [P, DK])
        bk_wide = sb(st, "bk_wide", [P, DK, P])
        w_landed = [sem(f"w_landed{i}") for i in range(5)]
        rows_landed = sem("rows_landed")
        set_hi = sem("set_hi")
        set_lo = sem("set_lo")
        wide_ready = sem("wide_ready")
        consts = sem("consts")
        prod_ready = sem("prod_ready")
        prod_hi = sem("prod_hi")
        prod_lo = sem("prod_lo")
        with nc.Block() as block:
            @block.sync
            def _(sp):
                sp.dma_start(raw_q[:], wq_t.rearrange("(k p) n -> p k n", p=P)).then_inc(w_landed[0], 16)
                sp.dma_start(raw_k[:], wk_t.rearrange("(k p) n -> p k n", p=P)).then_inc(w_landed[1], 16)
                sp.dma_start(bq_col[:], bq.rearrange("(k p) -> p k", p=P),
                             allow_slow_non_contiguous=True).then_inc(w_landed[4], 16)
                sp.dma_start(bk_col[:], bk.rearrange("(k p) -> p k", p=P),
                             allow_slow_non_contiguous=True).then_inc(w_landed[4], 16)
                sp.dma_start(raw[:], wqkv_t.rearrange("(k p) n -> p k n", p=P)).then_inc(w_landed[2], 16)
                sp.dma_start(raw_o[:], wo_t.rearrange("(k p) n -> p k n", p=P)).then_inc(w_landed[3], 16)
                sp.dma_start(qkvb_row[:], qkv_b.partition_broadcast(P)).then_inc(rows_landed, 16)
                sp.dma_start(ob_row[:], out_b.partition_broadcast(P)).then_inc(rows_landed, 16)
                sp.wait_ge(rows_landed, 32)

            @block.gpsimd
            def _(pool):
                nc.gpsimd.memset(ident[:], 0.0).then_inc(consts, 1)
                nc.gpsimd.memset(band[:], 1.0).then_inc(consts, 1)
                nc.gpsimd.memset(mhalf[:], -0.5).then_inc(consts, 1)
                nc.gpsimd.memset(half[:], 0.5).then_inc(consts, 1)
                nc.gpsimd.memset(ones[:], 1.0).then_inc(consts, 1)
                pool.wait_ge(consts, 5)
                nc.gpsimd.affine_select(out=ident[:], in_=ident[:], compare_op=ALU.not_equal, fill=1.0,
                                        base=0, pattern=[[-1, P]], channel_multiplier=1).then_inc(consts, 1)
                nc.gpsimd.affine_select(out=band[:], in_=band[:], compare_op=ALU.is_ge, fill=0.0,
                                        base=0, pattern=[[1, WIN]], channel_multiplier=-1).then_inc(consts, 1)
                pool.wait_ge(consts, 7)
                nc.gpsimd.affine_select(out=band[:], in_=band[:], compare_op=ALU.is_ge, fill=0.0,
                                        base=2 * HALO, pattern=[[-1, WIN]], channel_multiplier=1)\
                    .then_inc(consts, 1)

            @block.scalar
            def _(act):
                for n, (src, hi) in enumerate(((raw_q, q_h), (raw_k, k_h), (raw, wqkv_h), (raw_o, wo_h))):
                    act.wait_ge(w_landed[n], 16)
                    nc.scalar.copy(hi[:], src[:]).then_inc(set_hi, 1)
                for m in range(DK):
                    act.wait_ge(prod_ready, m + 1)
                    nc.scalar.copy(wp_h[:, m, :], score[:, m, :]).then_inc(prod_hi, 1)

            @block.vector
            def _(dve):
                dve.wait_ge(w_landed[4], 32)
                nc.vector.tensor_copy(bk_wide[:], bk_col[:].unsqueeze(2).to_broadcast([P, DK, P]))\
                    .then_inc(wide_ready, 1)
                for n, (src, hi, lo) in enumerate(((raw_q, q_h, q_l), (raw_k, k_h, k_l),
                                                   (raw, wqkv_h, wqkv_l), (raw_o, wo_h, wo_l))):
                    dve.wait_ge(set_hi, n + 1)
                    nc.vector.tensor_tensor(lo[:], src[:], hi[:].bitcast(F32), ALU.subtract).then_inc(set_lo, 1)
                for m in range(DK):
                    dve.wait_ge(prod_hi, m + 1)
                    nc.vector.tensor_tensor(wp_l[:, m, :], score[:, m, :], wp_h[:, m, :].bitcast(F32),
                                            ALU.subtract).then_inc(prod_lo, 1)
                dve.wait_ge(prod_ready, DK + 1)
                nc.vector.tensor_copy(wqb_row[:], work[:, 0, :]).then_inc(prod_lo, 1)
                nc.vector.tensor_copy(bqp[:], work[:, 1, 0:DK]).then_inc(prod_lo, 1)
                nc.vector.tensor_copy(bqbk[:], work[:, 2, 0:1]).then_inc(prod_lo, 1)

            @block.tensor
            def _(pe):
                pe.wait_ge(set_lo, 2)
                for m in range(DK):
                    for e in range(DK):
                        last = three(nc.tensor, score[:, m, :], q_h[:, e, P * m:P * m + P],
                                     q_l[:, e, P * m:P * m + P], k_h[:, e, :], k_l[:, e, :],
                                     e == 0, e == DK - 1)
                    last.then_inc(prod_ready, 1)
                pe.wait_ge(wide_ready, 1)
                for e in range(DK):
                    nc.tensor.matmul(work[:, 0, :], bk_wide[:, e, :], raw_q[:, e, :],
                                     start=e == 0, stop=e == DK - 1)
                for e in range(DK):
                    nc.tensor.matmul(work[:, 2, 0:1], bk_wide[:, e, :], bq_col[:, e:e + 1],
                                     start=e == 0, stop=e == DK - 1)
                for m in range(DK):
                    for e in range(DK):
                        last = nc.tensor.matmul(work[:, 1, m:m + 1], raw_k[:, e, P * m:P * m + P],
                                                bq_col[:, e:e + 1], start=e == 0, stop=e == DK - 1)
                last.then_inc(prod_ready, 1)

    xs = sb(scope, "xs", [P, 2, ST, D])
    xn = sb(scope, "xn", [P, 2, D])
    xt_h = sb(scope, "xt_h", [P, DK, SEQ], F32R)
    xt_l = sb(scope, "xt_l", [P, DK, SEQ], F32R)
    qk = sb(scope, "qk", [P, ST, 2 * D])
    v = sb(scope, "v", [P, ST, D])
    qbd_h = sb(scope, "qbd_h", [P, 2, HPG, SEQ], F32R)
    qbd_l = sb(scope, "qbd_l", [P, 2, HPG, SEQ], F32R)
    kt_h = sb(scope, "kt_h", [P, 2, SEQ], F32R)
    kt_l = sb(scope, "kt_l", [P, 2, SEQ], F32R)
    probs = sb(scope, "probs", [P, 2, HPG, WIN])
    sq = sb(scope, "sq", [P, 2 * D])
    stats = sb(scope, "stats", [P, ST, 6])
    mv = sb(scope, "mv", [P, ST, 2])
    ve = sb(scope, "ve", [P, ST])
    rstd = sb(scope, "rstd", [P, ST])
    ss = sb(scope, "ss", [P, 2 * H])
    nrm = sb(scope, "nrm", [P, 2 * H])
    rnrm = sb(scope, "rnrm", [P, 2 * H])
    qp = v
    rsum, o_sc = sq[:, 0:SEQ], sq[:, SEQ:2 * SEQ]

    uses = [("xt", t) for t in range(ST)] + [("qkv", t, j) for t in range(ST) for j in range(3)]
    uses += [(w, g) for g in range(HG) for w in ("kt", "qt")]
    uses += [("op", 0), ("op", 1), ("x2t", 0), ("op", 2), ("x2t", 1), ("op", 3), ("x2t", 2), ("x2t", 3)]
    uses += [("qp", m) for m in range(DK)]
    NU = len(uses)
    assert NU % 2 == 0
    use = {u: n for n, u in enumerate(uses)}
    read = {u: n + 3 for n, u in enumerate(uses)}

    x_landed = [sem(f"x_landed{i}") for i in range(2)]
    filled = sem("work_filled")
    released = sem("work_released")
    bd_zero = sem("bd_zero")
    st_done = sem("st_done")
    ag_done = sem("ag_done")
    ve_done = sem("ve_done")
    rstd_done = sem("rstd_done")
    xn_done = sem("xn_done")
    xb_done = sem("xb_done")
    xt_hi = sem("xt_hi")
    xt_lo = sem("xt_lo")
    sq_done = sem("sq_done")
    ss_done = sem("ss_done")
    nrm_done = sem("nrm_done")
    rn_done = sem("rn_done")
    qk_done = sem("qk_done")
    kq_hi = sem("kq_hi")
    kq_lo = sem("kq_lo")
    s_ready = sem("s_ready")
    exp_done = sem("exp_done")
    p_ready = sem("p_ready")
    pv_done = sem("pv_done")
    rs_done = sem("rs_done")
    os_done = sem("os_done")
    ot_hi = sem("ot_hi")
    ot_lo = sem("ot_lo")
    st2_done = sem("st2_done")
    ag2_done = sem("ag2_done")
    ve2_done = sem("ve2_done")
    rstd2_done = sem("rstd2_done")
    xn2_done = sem("xn2_done")
    c_done = sem("c_done")
    xt2_hi = sem("xt2_hi")
    xt2_lo = sem("xt2_lo")
    cb_done = sem("cb_done")
    x1_stored = [sem(f"x1_stored{i}") for i in range(2)]
    qp_stored = sem("qp_stored")

    units = [(g, i) for g in range(HG) for i in range(ST)]
    NUN = len(units)

    def window(i):
        lo, hi = max(0, P * i - HALO), min(SEQ, P * i + P + HALO)
        return lo, hi - lo, lo - (P * i - HALO)

    x_v = x.rearrange("(s t p) d -> s p t d", t=ST, p=P)
    x1_v = x1_dram.rearrange("(s t p) d -> s p t d", t=ST, p=P)
    qp_v = qp_dram.rearrange("(s t) p n -> s p t n", t=ST)

    with nc.Block() as block:
        @block.sync
        def _(sp):
            for par in range(2):
                sp.dma_start(xs[:, par], x_v[par]).then_inc(x_landed[par], 16)
            for s in range(2 * NB):
                par = s % 2
                sp.wait_ge(released, s * NU + read[("op", ST - 1)])
                sp.dma_start(x1_v[s], xs[:, par]).then_inc(x1_stored[par], 16)
                sp.wait_ge(released, s * NU + read[("qp", DK - 1)])
                sp.dma_start(qp_v[s], qp[:]).then_inc(qp_stored, 16)
                if s + 2 < 2 * NB:
                    sp.wait_ge(x1_stored[par], s // 2 * 16 + 16)
                    sp.wait_ge(xn2_done, s * ST + ST)
                    sp.dma_start(xs[:, par], x_v[s + 2]).then_inc(x_landed[par], 16)
            for par in range(2):
                sp.wait_ge(x1_stored[par], 16 * NB)
            sp.wait_ge(qp_stored, 32 * NB)

        @block.gpsimd
        def _(pool):
            nc.gpsimd.memset(qbd_h[:].bitcast(F32), 0.0).then_inc(bd_zero, 1)
            nc.gpsimd.memset(qbd_l[:].bitcast(F32), 0.0).then_inc(bd_zero, 1)
            with pool.Fori(0, NB) as b:
                for par in range(2):
                    s = b * 2 + par
                    pool.wait_ge(ve_done, s + 1)
                    nc.gpsimd.tensor_tensor(rstd[:], ve[:], mhalf[:, 0:ST], ALU.pow).then_inc(rstd_done, 1)
                    for t in range(ST):
                        pool.wait_ge(ss_done, s * ST + t + 1)
                        nc.gpsimd.tensor_tensor(nrm[:], ss[:], half[:], ALU.pow).then_inc(nrm_done, 1)
                    pool.wait_ge(xn_done, s * ST + ST)
                    nc.gpsimd.tensor_tensor(xs[:, par], xs[:, par],
                                            ob_row[:].unsqueeze(1).to_broadcast([P, ST, D]), ALU.add)\
                        .then_inc(xb_done, 1)
                    for n, (g, i) in enumerate(units):
                        lo, w, c0 = window(i)
                        pool.wait_ge(exp_done, s * NUN + n + 1)
                        nc.gpsimd.tensor_tensor(probs[:, n % 2, :, 0:w], probs[:, n % 2, :, 0:w],
                                                band[:, c0:c0 + w].unsqueeze(1).to_broadcast([P, HPG, w]),
                                                ALU.mult).then_inc(p_ready, 1)
                    for t in range(ST):
                        pool.wait_ge(ve2_done, s * ST + t + 1)
                        nc.gpsimd.tensor_tensor(rstd[:, t:t + 1], ve[:, t:t + 1], mhalf[:, 0:1], ALU.pow)\
                            .then_inc(rstd2_done, 1)

        @block.scalar
        def _(act):
            act.wait_ge(bd_zero, 2)
            with act.Fori(0, NB) as b:
                for par in range(2):
                    s = b * 2 + par

                    def hi_tile(kind, t, done):
                        act.wait_ge(filled, s * NU + use[(kind, t)] + 1)
                        nc.scalar.copy(xt_h[:, :, P * t:P * t + P],
                                       work[:, use[(kind, t)] % 2, :].rearrange("p (k c) -> p k c", k=DK))\
                            .then_inc(done, 1)

                    def key_hi(g):
                        act.wait_ge(filled, s * NU + use[("kt", g)] + 1)
                        nc.scalar.copy(kt_h[:, g % 2, :], work[:, use[("kt", g)] % 2, :]).then_inc(kq_hi, 1)

                    def query_hi(g, h):
                        act.wait_ge(filled, s * NU + use[("qt", g)] + 1)
                        r = slice(DH * h, DH * h + DH)
                        nc.scalar.copy(qbd_h[r, g % 2, h, :], work[r, use[("qt", g)] % 2, :]).then_inc(kq_hi, 1)

                    def exp(n):
                        g, i = units[n]
                        lo, w, c0 = window(i)
                        act.wait_ge(s_ready, s * NUN + n + 1)
                        if n >= 2:
                            act.wait_ge(pv_done, s * NUN + n - 1)
                        b0 = 2 * (n % 2)
                        nc.scalar.activation(
                            probs[:, n % 2].rearrange("p (a h) w -> p a h w", a=2)[:, :, :, 0:w],
                            score[:, b0:b0 + 2, 0:2 * WIN].rearrange("p a (h w) -> p a h w", h=2)[:, :, :, 0:w],
                            ACT.Exp).then_inc(exp_done, 1)

                    def out_hi(g):
                        act.wait_ge(os_done, s * HG + g + 1)
                        nc.scalar.copy(xt_h[:, g, :], o_sc).then_inc(ot_hi, 1)

                    for t in range(ST):
                        hi_tile("xt", t, xt_hi)
                    for t in range(ST):
                        act.wait_ge(released, s * NU + read[("qkv", t, 1)])
                        if t:
                            act.wait_ge(ss_done, s * ST + t)
                        nc.scalar.activation(sq[:], qk[:, t, :], ACT.Square).then_inc(sq_done, 1)
                    key_hi(0)
                    for h in range(HPG):
                        query_hi(0, h)
                    exp(0)
                    exp(1)
                    for n, (g, i) in enumerate(units):
                        if i == 0 and g >= 1:
                            out_hi(g - 1)
                        if g + 1 < HG:
                            if i == 0:
                                key_hi(g + 1)
                                query_hi(g + 1, 0)
                                query_hi(g + 1, 1)
                            if i == 1:
                                query_hi(g + 1, 2)
                                query_hi(g + 1, 3)
                        if n + 2 < NUN:
                            exp(n + 2)
                    out_hi(HG - 1)
                    for t in range(ST):
                        hi_tile("x2t", t, xt2_hi)

        @block.vector
        def _(dve):
            V = nc.vector
            V.memset(stats[:, 0, :], 0.0).then_inc(released, 1)
            V.memset(stats[:, 1, :], 0.0).then_inc(released, 1)
            dve.wait_ge(released, 2)
            dve.wait_ge(bd_zero, 2)
            with dve.Fori(0, NB) as b:
                for par in range(2):
                    s = b * 2 + par

                    def lo_tile(kind, t, hi_sem, lo_sem):
                        dve.wait_ge(hi_sem, s * ST + t + 1)
                        V.tensor_tensor(xt_l[:, :, P * t:P * t + P],
                                        work[:, use[(kind, t)] % 2, :].rearrange("p (k c) -> p k c", k=DK),
                                        xt_h[:, :, P * t:P * t + P].bitcast(F32), ALU.subtract)\
                            .then_inc(released, 1)

                    dve.wait_ge(x_landed[par], b * 16 + 16)
                    for t in range(ST):
                        V.bn_stats(stats[:, t, :], xs[:, par, t, :]).then_inc(st_done, 1)
                    dve.wait_ge(st_done, s * ST + ST)
                    V.memset(wait_pad[:, 0:1], 0.0)
                    for t in range(ST):
                        V.bn_aggr(mv[:, t, :], stats[:, t, :]).then_inc(ag_done, 1)
                    dve.wait_ge(ag_done, s * ST + ST)
                    V.tensor_scalar(ve[:], mv[:, :, 1], LN_EPS, None, ALU.add).then_inc(ve_done, 1)
                    dve.wait_ge(rstd_done, s + 1)

                    def norm1(t):
                        if t >= 2:
                            dve.wait_ge(filled, s * NU + use[("xt", t - 2)] + 1)
                        V.tensor_scalar(xn[:, t % 2, :], xs[:, par, t, :], mv[:, t, 0:1], rstd[:, t:t + 1],
                                        ALU.subtract, ALU.mult).then_inc(xn_done, 1)

                    norm1(0)
                    norm1(1)
                    for t in range(ST):
                        if t + 2 < ST:
                            norm1(t + 2)
                        lo_tile("xt", t, xt_hi, xt_lo)
                    def unit(t):
                        dve.wait_ge(sq_done, s * ST + t + 1)
                        if t:
                            dve.wait_ge(nrm_done, s * ST + t)
                        V.tensor_reduce(ss[:], sq[:].rearrange("p (h d) -> p h d", d=DH), AX.X, ALU.add)\
                            .then_inc(ss_done, 1)
                        dve.wait_ge(nrm_done, s * ST + t + 1)
                        V.tensor_scalar(rnrm[:], nrm[:], NORM_EPS, None, ALU.add).then_inc(rn_done, 1)
                        dve.wait_ge(rn_done, s * 2 * ST + 2 * t + 1)
                        V.reciprocal(rnrm[:], rnrm[:]).then_inc(rn_done, 1)
                        dve.wait_ge(rn_done, s * 2 * ST + 2 * t + 2)
                        q3 = qk[:, t, :].rearrange("p (h d) -> p h d", d=DH)
                        V.tensor_tensor(q3, q3, rnrm[:].unsqueeze(2).to_broadcast([P, 2 * H, DH]), ALU.mult)\
                            .then_inc(qk_done, 1)

                    for t in range(ST):
                        for j in range(3):
                            u = use[("qkv", t, j)]
                            dve.wait_ge(filled, s * NU + u + 1)
                            if t == 0 and j == 2:
                                dve.wait_ge(qp_stored, s * 16)
                            dst = v[:, t, :] if j == 2 else qk[:, t, D * j:D * j + D]
                            V.tensor_tensor(dst, work[:, u % 2, :], qkvb_row[:, D * j:D * j + D], ALU.add)\
                                .then_inc(released, 1)
                        unit(t)

                    def key_lo(g):
                        dve.wait_ge(kq_hi, s * 5 * HG + 5 * g + 1)
                        V.tensor_tensor(kt_l[:, g % 2, :], work[:, use[("kt", g)] % 2, :],
                                        kt_h[:, g % 2, :].bitcast(F32), ALU.subtract).then_inc(released, 1)

                    def query_lo(g, h):
                        dve.wait_ge(kq_hi, s * 5 * HG + 5 * g + 2 + h)
                        r = slice(DH * h, DH * h + DH)
                        last = V.tensor_tensor(qbd_l[r, g % 2, h, :], work[r, use[("qt", g)] % 2, :],
                                               qbd_h[r, g % 2, h, :].bitcast(F32), ALU.subtract)
                        last.then_inc(released if h == HPG - 1 else kq_lo, 1)

                    key_lo(0)
                    for h in range(HPG):
                        query_lo(0, h)
                    for g in range(HG):
                        if g + 1 < HG:
                            key_lo(g + 1)
                            for h in range(HPG):
                                query_lo(g + 1, h)
                        dve.wait_ge(pv_done, s * NUN + ST * g + ST)
                        V.reciprocal(rsum, work[:, 3, :]).then_inc(rs_done, 1)
                        dve.wait_ge(rs_done, s * HG + g + 1)
                        V.tensor_tensor(o_sc, work[:, 2, :], rsum, ALU.mult).then_inc(os_done, 1)
                        dve.wait_ge(ot_hi, s * HG + g + 1)
                        V.tensor_tensor(xt_l[:, g, :], o_sc, xt_h[:, g, :].bitcast(F32), ALU.subtract)\
                            .then_inc(ot_lo, 1)

                    dve.wait_ge(xb_done, s + 1)

                    def residual(t):
                        u = use[("op", t)]
                        dve.wait_ge(filled, s * NU + u + 1)
                        V.tensor_tensor(xs[:, par, t, :], work[:, u % 2, :], xs[:, par, t, :], ALU.add)\
                            .then_inc(released, 1)
                        dve.wait_ge(released, s * NU + read[("op", t)])

                    def norm2(t):
                        k = s * ST + t + 1
                        V.bn_stats(stats[:, t, :], xs[:, par, t, :]).then_inc(st2_done, 1)
                        dve.wait_ge(st2_done, k)
                        V.memset(wait_pad[:, 1 + t:2 + t], 0.0)
                        V.bn_aggr(mv[:, t, :], stats[:, t, :]).then_inc(ag2_done, 1)
                        dve.wait_ge(ag2_done, k)
                        V.tensor_scalar(ve[:, t:t + 1], mv[:, t, 1:2], LN_EPS, None, ALU.add).then_inc(ve2_done, 1)
                        dve.wait_ge(rstd2_done, k)
                        if t >= 2:
                            dve.wait_ge(filled, s * NU + use[("x2t", t - 2)] + 1)
                            dve.wait_ge(c_done, k - 2)
                        V.tensor_scalar(xn[:, t % 2, :], xs[:, par, t, :], mv[:, t, 0:1], rstd[:, t:t + 1],
                                        ALU.subtract, ALU.mult).then_inc(xn2_done, 1)
                        dve.wait_ge(xn2_done, k)
                        V.scalar_tensor_tensor(rsum, xn[:, t % 2, :], 1.0, wqb_row[:], ALU.mult, ALU.mult,
                                               accum_out=ve[:, t:t + 1]).then_inc(c_done, 1)
                        dve.wait_ge(c_done, k)

                    residual(0)
                    norm2(0)
                    residual(1)
                    norm2(1)
                    lo_tile("x2t", 0, xt2_hi, xt2_lo)
                    residual(2)
                    norm2(2)
                    lo_tile("x2t", 1, xt2_hi, xt2_lo)
                    residual(3)
                    norm2(3)
                    lo_tile("x2t", 2, xt2_hi, xt2_lo)
                    lo_tile("x2t", 3, xt2_hi, xt2_lo)
                    V.tensor_scalar(q_const[:, bass.ds(s * ST, ST)], ve[:], bqbk[:, 0:1], None, ALU.add)\
                        .then_inc(cb_done, 1)
                    dve.wait_ge(cb_done, s + 1)
                    for m in range(DK):
                        u = use[("qp", m)]
                        dve.wait_ge(filled, s * NU + u + 1)
                        V.tensor_scalar(qp[:].rearrange("p t (m c) -> p t m c", m=DK)[:, :, m, :],
                                        work[:, u % 2, :].rearrange("p (t c) -> p t c", t=ST),
                                        bqp[:, m:m + 1], None, ALU.add).then_inc(released, 1)

        @block.tensor
        def _(pe):
            PE = nc.tensor
            with pe.Fori(0, NB) as b:
                for par in range(2):
                    s = b * 2 + par

                    def bank(u):
                        pe.wait_ge(released, s * NU + u + 1)
                        return work[:, u % 2, :]

                    def transposes(kind, t, done):
                        out = bank(use[(kind, t)])
                        pe.wait_ge(done, s * ST + t + 1)
                        for k in range(DK):
                            last = PE.transpose(out[:, P * k:P * k + P], xn[:, t % 2, P * k:P * k + P], ident[:])
                        last.then_inc(filled, 1)

                    for t in range(ST):
                        transposes("xt", t, xn_done)
                    for t in range(ST):
                        if t == 0:
                            pe.wait_ge(released, s * NU + read[("xt", ST - 1)])
                        for j in range(3):
                            out = bank(use[("qkv", t, j)])
                            for k in range(DK):
                                last = three(PE, out, xt_h[:, k, P * t:P * t + P], xt_l[:, k, P * t:P * t + P],
                                             wqkv_h[:, k, D * j:D * j + D], wqkv_l[:, k, D * j:D * j + D],
                                             k == 0, k == DK - 1)
                            last.then_inc(filled, 1)
                    pe.wait_ge(qk_done, s * ST + ST)

                    def head_transposes(g):
                        for kind, off in (("kt", D), ("qt", 0)):
                            out = bank(use[(kind, g)])
                            for t in range(ST):
                                last = PE.transpose(out[:, P * t:P * t + P],
                                                    qk[:, t, off + P * g:off + P * g + P], ident[:])
                            last.then_inc(filled, 1)

                    def scores(n):
                        g, i = units[n]
                        lo, w, c0 = window(i)
                        if i == 0:
                            pe.wait_ge(released, s * NU + read[("qt", g)])
                        if n >= 2:
                            pe.wait_ge(exp_done, s * NUN + n - 1)
                        for a in range(2):
                            out = score[:, 2 * (n % 2) + a, 0:2 * WIN].rearrange("p (h w) -> p h w", h=2)[:, :, 0:w]
                            last = three(PE, out, kt_h[:, g % 2, P * i:P * i + P], kt_l[:, g % 2, P * i:P * i + P],
                                         qbd_h[:, g % 2, 2 * a:2 * a + 2, lo:lo + w],
                                         qbd_l[:, g % 2, 2 * a:2 * a + 2, lo:lo + w], True, True)
                        last.then_inc(s_ready, 1)

                    def weighted(n):
                        g, i = units[n]
                        lo, w, c0 = window(i)
                        pe.wait_ge(p_ready, s * NUN + n + 1)
                        if i == 0 and g:
                            pe.wait_ge(os_done, s * HG + g)
                        for h in range(HPG):
                            r = slice(DH * h, DH * h + DH)
                            PE.matmul(work[r, 2, lo:lo + w], v[:, i, P * g + DH * h:P * g + DH * h + DH],
                                      probs[:, n % 2, h, 0:w], start=i == 0, stop=i == ST - 1,
                                      skip_group_check=True)
                        for h in range(HPG):
                            r = slice(DH * h, DH * h + DH)
                            last = PE.matmul(work[r, 3, lo:lo + w], ones[:], probs[:, n % 2, h, 0:w],
                                             start=i == 0, stop=i == ST - 1, skip_group_check=True)
                        last.then_inc(pv_done, 1)

                    head_transposes(0)
                    scores(0)
                    scores(1)
                    for n, (g, i) in enumerate(units):
                        if i == 0 and g + 1 < HG:
                            head_transposes(g + 1)
                        weighted(n)
                        if n + 2 < NUN:
                            scores(n + 2)

                    def project(t):
                        if t == 0:
                            pe.wait_ge(ot_lo, s * HG + HG)
                        out = bank(use[("op", t)])
                        for g in range(HG):
                            last = three(PE, out, xt_h[:, g, P * t:P * t + P], xt_l[:, g, P * t:P * t + P],
                                         wo_h[:, g, :], wo_l[:, g, :], g == 0, g == HG - 1)
                        last.then_inc(filled, 1)

                    project(0)
                    project(1)
                    transposes("x2t", 0, xn2_done)
                    project(2)
                    transposes("x2t", 1, xn2_done)
                    project(3)
                    transposes("x2t", 2, xn2_done)
                    transposes("x2t", 3, xn2_done)
                    pe.wait_ge(released, s * NU + read[("x2t", ST - 1)])
                    for m in range(DK):
                        out = bank(use[("qp", m)])
                        for k in range(DK):
                            last = three(PE, out, wp_h[:, k, P * m:P * m + P], wp_l[:, k, P * m:P * m + P],
                                         xt_h[:, k, :], xt_l[:, k, :], k == 0, k == DK - 1)
                        last.then_inc(filled, 1)


def cross_phase(nc, scope, sb, sem, score, work, ident, q_const,
                ctx_n, ctx_t, wv, bv, x1_dram, qp_dram, x2_dram):
    cn_h = sb(scope, "cn_h", [P, CK, D], F32R)
    cn_l = sb(scope, "cn_l", [P, CK, D], F32R)
    ct_h = sb(scope, "ct_h", [P, DK, CTX], F32R)
    ct_l = sb(scope, "ct_l", [P, DK, CTX], F32R)
    wv_h = sb(scope, "wv_h", [P, DK, D], F32R)
    wv_l = sb(scope, "wv_l", [P, DK, D], F32R)
    bv_row = sb(scope, "bv_row", [P, D])
    stage = sb(scope, "stage", [P, 2, 1024])
    q_raw = sb(scope, "q_raw", [P, D])
    q_h = sb(scope, "q_h", [P, 2, D], F32R)
    q_l = sb(scope, "q_l", [P, 2, D], F32R)
    pr = sb(scope, "pr", [P, CTX])
    pt_h = sb(scope, "pt_h", [P, CK, P], F32R)
    pt_l = sb(scope, "pt_l", [P, CK, P], F32R)
    o = sb(scope, "o", [P, D])
    ot_h = sb(scope, "ot_h", [P, D], F32R)
    ot_l = sb(scope, "ot_l", [P, D], F32R)
    xr = sb(scope, "xr", [P, 2, D])
    mx = sb(scope, "mx", [P, 4])
    negm = sb(scope, "negm", [P, 2])
    shift = sb(scope, "shift", [P, 2])
    sums = sb(scope, "sums", [P, 4])
    rinv = sb(scope, "rinv", [P, 2])

    SB = CTX // 512
    NCH = 16
    staged = [sem(f"ctx_staged{i}") for i in range(2)]
    ctx_hi = sem("ctx_hi")
    ctx_lo = sem("ctx_lo")
    wv_staged = [sem(f"wv_staged{i}") for i in range(2)]
    wv_hi = sem("wv_hi")
    wv_lo = sem("wv_lo")
    bv_landed = sem("bv_landed")
    q_landed = sem("q_landed")
    q_hi = sem("xq_hi")
    q_lo = sem("xq_lo")
    sc_ready = sem("xs_ready")
    mx_done = sem("mx_done")
    m_done = sem("m_done")
    negm_done = sem("negm_done")
    shift_done = sem("shift_done")
    e_done = sem("e_done")
    sum_done = sem("sum_done")
    rinv_done = sem("rinv_done")
    pt_ready = sem("pt_ready")
    pth_done = sem("pth_done")
    ptl_done = sem("ptl_done")
    o_ready = sem("o_ready")
    o_done = sem("o_done")
    tr_ready = sem("tr_ready")
    oth_done = sem("oth_done")
    otl_done = sem("otl_done")
    y_ready = sem("y_ready")
    x2_done = sem("x2_done")
    xr_landed = [sem(f"xr_landed{i}") for i in range(2)]
    xb_done = sem("xbv_done")
    x2_stored = [sem(f"x2_stored{i}") for i in range(2)]

    ct_v = ctx_t.rearrange("b (k p) n -> b p k n", p=P)
    cn_v = ctx_n.rearrange("b (t p) d -> b p t d", p=P)

    def piece(c):
        if c < 8:
            return (ct_h[:, :, 256 * c:256 * c + 256], ct_l[:, :, 256 * c:256 * c + 256], DK)
        return cn_h[:, 2 * (c - 8):2 * (c - 8) + 2, :], cn_l[:, 2 * (c - 8):2 * (c - 8) + 2, :], 2

    def tiles(eng, body):
        body(0, 0, 0, True, False)
        with eng.Fori(0, (BT - 2) // 2) as j:
            body(j * 2 + 1, 1, j, False, False)
            body(j * 2 + 2, 0, j + 1, False, False)
        body(BT - 1, 1, BT // 2 - 1, False, True)

    with nc.Block() as block:
        @block.sync
        def _(sp):
            wv_v = wv.rearrange("(k p) n -> p k n", p=P)
            for i in range(2):
                sp.dma_start(stage[:, i, :].rearrange("p (k n) -> p k n", k=2), wv_v[:, 2 * i:2 * i + 2, :])\
                    .then_inc(wv_staged[i], 16)
            sp.dma_start(bv_row[:], bv.partition_broadcast(P)).then_inc(bv_landed, 16)
            with sp.Fori(0, NB) as b:
                sp.wait_ge(q_lo, b * BT)
                sp.dma_start(q_raw[:], qp_dram[bass.ds(b * BT, 1)].rearrange("a p n -> (a p) n"))\
                    .then_inc(q_landed, 16)
                for c in range(NCH):
                    if c < 2:
                        sp.wait_ge(wv_lo, c + 1)
                    if c < 2:
                        sp.wait_ge(ctx_lo, b * NCH)
                    else:
                        sp.wait_ge(ctx_lo, b * NCH + c - 1)
                    _, _, k = piece(c)
                    dst = stage[:, c % 2, :].rearrange("p (k n) -> p k n", k=k)
                    if c < 8:
                        src = ct_v[bass.ds(b, 1), :, :, 256 * c:256 * c + 256]
                    else:
                        src = cn_v[bass.ds(b, 1), :, 2 * (c - 8):2 * (c - 8) + 2, :]
                    sp.dma_start(dst, src.rearrange("a p k n -> (a p) k n")).then_inc(staged[c % 2], 16)

                def load(t, par, before, first, last):
                    g = b * BT + t
                    if not last:
                        sp.wait_ge(q_lo, g + 1)
                        sp.dma_start(q_raw[:], qp_dram[bass.ds(g + 1, 1)].rearrange("a p n -> (a p) n"))\
                            .then_inc(q_landed, 16)
                    sp.wait_ge(x2_stored[par], (b * (BT // 2) + before) * 16)
                    sp.dma_start(xr[:, par, :], x1_dram[bass.ds(g * P, P), :]).then_inc(xr_landed[par], 16)
                    if not first:
                        sp.wait_ge(x2_done, g)
                        sp.dma_start(x2_dram[bass.ds((g - 1) * P, P), :], xr[:, 1 - par, :])\
                            .then_inc(x2_stored[1 - par], 16)
                    if last:
                        sp.wait_ge(x2_done, g + 1)
                        sp.dma_start(x2_dram[bass.ds(g * P, P), :], xr[:, par, :]).then_inc(x2_stored[par], 16)

                tiles(sp, load)
            for i in range(2):
                sp.wait_ge(x2_stored[i], NB * BT // 2 * 16)

        @block.gpsimd
        def _(pool):
            pool.wait_ge(bv_landed, 16)
            with pool.Fori(0, NB) as b:
                def body(t, par, before, first, last):
                    g = b * BT + t
                    pool.wait_ge(xr_landed[par], (b * (BT // 2) + before) * 16 + 16)
                    nc.gpsimd.tensor_tensor(xr[:, par, :], xr[:, par, :], bv_row[:], ALU.add).then_inc(xb_done, 1)
                tiles(pool, body)

        @block.scalar
        def _(act):
            for i in range(2):
                act.wait_ge(wv_staged[i], 16)
                nc.scalar.copy(wv_h[:, 2 * i:2 * i + 2, :], stage[:, i, :].rearrange("p (k n) -> p k n", k=2))\
                    .then_inc(wv_hi, 1)
            with act.Fori(0, NB) as b:
                def q_high(g, par):
                    act.wait_ge(q_landed, g * 16 + 16)
                    nc.scalar.copy(q_h[:, par, :], q_raw[:]).then_inc(q_hi, 1)

                for c in range(NCH):
                    hi, lo, k = piece(c)
                    act.wait_ge(staged[c % 2], b * (NCH // 2) * 16 + 16 * (c // 2) + 16)
                    if c == 0:
                        act.wait_ge(sc_ready, b * BT * SB)
                    if c == 8:
                        act.wait_ge(o_ready, b * BT)
                    nc.scalar.copy(hi, stage[:, c % 2, :].rearrange("p (k n) -> p k n", k=k)).then_inc(ctx_hi, 1)
                    if c == 1:
                        q_high(b * BT, 0)

                def exps(t, par):
                    g = b * BT + t
                    act.wait_ge(shift_done, g + 1)
                    act.wait_ge(pt_ready, g * 4)
                    act.wait_ge(sum_done, g)
                    for c in range(SB):
                        nc.scalar.activation(pr[:, 512 * c:512 * c + 512], score[:, c, :], ACT.Exp,
                                             bias=shift[:, par:par + 1], accum_out=sums[:, c:c + 1])\
                            .then_inc(e_done, 1)

                def finish(t, par):
                    g = b * BT + t
                    act.wait_ge(tr_ready, g + 1)
                    nc.scalar.copy(ot_h[:], work[:, 3, :]).then_inc(oth_done, 1)

                def body(t, par, before, first, last):
                    g = b * BT + t
                    if first:
                        exps(t, par)
                    if not last:
                        q_high(g + 1, 1 - par)
                    for c in range(4):
                        act.wait_ge(pt_ready, g * 4 + c + 1)
                        nc.scalar.copy(pt_h[:, 4 * c:4 * c + 4, :],
                                       work[:, c % 2, :].rearrange("p (k q) -> p k q", q=P)).then_inc(pth_done, 1)
                        if c == 1 and not first:
                            finish(t - 1, 1 - par)
                    if not last:
                        exps(t + 1, 1 - par)
                    act.wait_ge(o_ready, g + 1)
                    act.wait_ge(rinv_done, g + 1)
                    nc.scalar.mul(o[:], work[:, 2, :], rinv[:, par:par + 1]).then_inc(o_done, 1)
                    if last:
                        finish(t, par)
                tiles(act, body)

        @block.vector
        def _(dve):
            V = nc.vector
            for i in range(2):
                dve.wait_ge(wv_hi, i + 1)
                V.tensor_tensor(wv_l[:, 2 * i:2 * i + 2, :], stage[:, i, :].rearrange("p (k n) -> p k n", k=2),
                                wv_h[:, 2 * i:2 * i + 2, :].bitcast(F32), ALU.subtract).then_inc(wv_lo, 1)
            with dve.Fori(0, NB) as b:
                def q_low(g, par):
                    dve.wait_ge(q_hi, g + 1)
                    V.tensor_tensor(q_l[:, par, :], q_raw[:], q_h[:, par, :].bitcast(F32), ALU.subtract)\
                        .then_inc(q_lo, 1)

                for c in range(NCH):
                    hi, lo, k = piece(c)
                    dve.wait_ge(ctx_hi, b * NCH + c + 1)
                    V.tensor_tensor(lo, stage[:, c % 2, :].rearrange("p (k n) -> p k n", k=k), hi.bitcast(F32),
                                    ALU.subtract).then_inc(ctx_lo, 1)
                    if c == 1:
                        q_low(b * BT, 0)

                def maxima(t, par, c):
                    g = b * BT + t
                    dve.wait_ge(sc_ready, g * SB + c + 1)
                    V.reduce_max(mx[:, c:c + 1], score[:, c, :], AX.X).then_inc(mx_done, 1)

                def shifts(t, par):
                    g = b * BT + t
                    dve.wait_ge(mx_done, g * SB + SB)
                    V.reduce_max(negm[:, par:par + 1], mx[:], AX.X).then_inc(m_done, 1)
                    dve.wait_ge(m_done, g + 1)
                    qc = q_const[:, bass.ds(g, 1)]
                    V.tensor_scalar(negm[:, par:par + 1], negm[:, par:par + 1], qc, -1.0, ALU.add, ALU.mult)\
                        .then_inc(negm_done, 1)
                    dve.wait_ge(negm_done, g + 1)
                    V.tensor_tensor(shift[:, par:par + 1], negm[:, par:par + 1], qc, ALU.add)\
                        .then_inc(shift_done, 1)

                def total(t, par):
                    g = b * BT + t
                    dve.wait_ge(e_done, g * SB + SB)
                    V.reduce_sum(rinv[:, par:par + 1], sums[:], AX.X).then_inc(sum_done, 1)
                    dve.wait_ge(sum_done, g + 1)
                    V.reciprocal(rinv[:, par:par + 1], rinv[:, par:par + 1]).then_inc(rinv_done, 1)

                def finish(t, par):
                    g = b * BT + t
                    dve.wait_ge(oth_done, g + 1)
                    V.tensor_tensor(ot_l[:], work[:, 3, :], ot_h[:].bitcast(F32), ALU.subtract).then_inc(otl_done, 1)

                def result(t, par):
                    g = b * BT + t
                    dve.wait_ge(y_ready, g + 1)
                    dve.wait_ge(xb_done, g + 1)
                    V.tensor_tensor(xr[:, par, :], work[:, 3, :], xr[:, par, :], ALU.add).then_inc(x2_done, 1)

                def body(t, par, before, first, last):
                    g = b * BT + t
                    if first:
                        for c in range(SB):
                            maxima(t, par, c)
                        shifts(t, par)
                        total(t, par)
                    if not last:
                        q_low(g + 1, 1 - par)
                    for c in range(4):
                        dve.wait_ge(pth_done, g * 4 + c + 1)
                        V.tensor_tensor(pt_l[:, 4 * c:4 * c + 4, :],
                                        work[:, c % 2, :].rearrange("p (k q) -> p k q", q=P),
                                        pt_h[:, 4 * c:4 * c + 4, :].bitcast(F32), ALU.subtract)\
                            .then_inc(ptl_done, 1)
                        if not last:
                            maxima(t + 1, 1 - par, c)
                        if c == 1 and not first:
                            finish(t - 1, 1 - par)
                        if c == 2 and not first:
                            result(t - 1, 1 - par)
                    if not last:
                        shifts(t + 1, 1 - par)
                        total(t + 1, 1 - par)
                    if last:
                        finish(t, par)
                        result(t, par)
                tiles(dve, body)

        @block.tensor
        def _(pe):
            PE = nc.tensor
            with pe.Fori(0, NB) as b:
                def scores(t, par, c):
                    g = b * BT + t
                    if c == 0:
                        pe.wait_ge(q_lo, g + 1)
                    if isinstance(t, int) and t == 0:
                        pe.wait_ge(ctx_lo, b * NCH + 2 * c + 2)
                    if not (isinstance(t, int) and t == 0):
                        pe.wait_ge(e_done, (g - 1) * SB + SB)
                    for k in range(DK):
                        last = three(PE, score[:, c, :], q_h[:, par, P * k:P * k + P], q_l[:, par, P * k:P * k + P],
                                     ct_h[:, k, 512 * c:512 * c + 512], ct_l[:, k, 512 * c:512 * c + 512],
                                     k == 0, k == DK - 1)
                    last.then_inc(sc_ready, 1)

                def transposes(t, c):
                    g = b * BT + t
                    pe.wait_ge(e_done, g * SB + c + 1)
                    if c >= 2:
                        pe.wait_ge(ptl_done, g * 4 + c - 1)
                    elif not (isinstance(t, int) and t == 0):
                        pe.wait_ge(ptl_done, (g - 1) * 4 + c + 3)
                    for k in range(4):
                        last = PE.transpose(work[:, c % 2, P * k:P * k + P],
                                            pr[:, 512 * c + P * k:512 * c + P * k + P], ident[:])
                    last.then_inc(pt_ready, 1)

                def turn(t):
                    g = b * BT + t
                    pe.wait_ge(o_done, g + 1)
                    pe.wait_ge(x2_done, g)
                    for k in range(DK):
                        last = PE.transpose(work[:, 3, P * k:P * k + P], o[:, P * k:P * k + P], ident[:])
                    last.then_inc(tr_ready, 1)

                def project(t):
                    g = b * BT + t
                    pe.wait_ge(otl_done, g + 1)
                    for k in range(DK):
                        last = three(PE, work[:, 3, :], ot_h[:, P * k:P * k + P], ot_l[:, P * k:P * k + P],
                                     wv_h[:, k, :], wv_l[:, k, :], k == 0, k == DK - 1)
                    last.then_inc(y_ready, 1)

                def body(t, par, before, first, last):
                    g = b * BT + t
                    if first:
                        for c in range(SB):
                            scores(t, par, c)
                    for c in range(4):
                        if not last:
                            scores(t + 1, 1 - par, c)
                        transposes(t, c)
                        if c == 1 and not first:
                            turn(t - 1)
                        if c == 2 and not first:
                            project(t - 1)
                    if first:
                        pe.wait_ge(ctx_lo, b * NCH + NCH)
                    else:
                        pe.wait_ge(o_done, g)
                    for kt in range(CK):
                        if kt % 4 == 0:
                            pe.wait_ge(ptl_done, g * 4 + kt // 4 + 1)
                        last_mm = three(PE, work[:, 2, :], pt_h[:, kt, :], pt_l[:, kt, :],
                                        cn_h[:, kt, :], cn_l[:, kt, :], kt == 0, kt == CK - 1)
                    last_mm.then_inc(o_ready, 1)
                    if last:
                        turn(t)
                        project(t)
                tiles(pe, body)


def ffn_phase(nc, scope, sb, sem, score, work, ident, mhalf, wait_pad, wg_t, wu_t, wd_t, x2_dram, out):
    wg_h = sb(scope, "wg_h", [P, DK, FH], F32R)
    wg_l = sb(scope, "wg_l", [P, DK, FH], F32R)
    wu_h = sb(scope, "wu_h", [P, DK, FH], F32R)
    wu_l = sb(scope, "wu_l", [P, DK, FH], F32R)
    wd_h = sb(scope, "wd_h", [P, FK, D], F32R)
    wd_l = sb(scope, "wd_l", [P, FK, D], F32R)
    stage = sb(scope, "w_stage", [P, 2, 3, 512], I32)
    xs = sb(scope, "fx", [P, ST, D])
    xn = sb(scope, "fxn", [P, 2, D])
    xt_h = sb(scope, "fxt_h", [P, DK, SEQ], F32R)
    xt_l = sb(scope, "fxt_l", [P, DK, SEQ], F32R)
    gate = sb(scope, "gate", [P, 2, SEQ])
    hid = sb(scope, "hid", [P, SEQ])
    hid_h = sb(scope, "hid_h", [P, 2, SEQ], F32R)
    hid_l = sb(scope, "hid_l", [P, 2, SEQ], F32R)
    stats = sb(scope, "fstats", [P, ST, 6])
    mv = sb(scope, "fmv", [P, ST, 2])
    ve = sb(scope, "fve", [P, ST])
    rstd = sb(scope, "frstd", [P, ST])

    w_staged = [[sem(f"w_staged{i}{j}") for j in range(3)] for i in range(2)]
    w_hi = sem("fw_hi")
    w_lo = sem("fw_lo")
    x_landed = sem("fx_landed")
    st_done = sem("fst_done")
    ag_done = sem("fag_done")
    ve_done = sem("fve_done")
    rstd_done = sem("frstd_done")
    xn_done = sem("fxn_done")
    xt_ready = sem("fxt_ready")
    xt_hi = sem("fxt_hi_done")
    xt_lo = sem("fxt_lo_done")
    gu_ready = sem("gu_ready")
    gate_done = sem("gate_done")
    hid_done = sem("hid_done")
    hidh_done = sem("hidh_done")
    hidl_done = sem("hidl_done")
    down_done = sem("down_done")
    y_done = sem("fy_done")
    stored = sem("fstored")

    x_v = x2_dram.rearrange("(s t p) d -> s p t d", t=ST, p=P)
    o_v = out.rearrange("(s t p) d -> s p t d", t=ST, p=P)
    wg_v = wg_t.rearrange("(k p) n -> p k n", p=P)
    wu_v = wu_t.rearrange("(k p) n -> p k n", p=P)
    wd_v = wd_t.rearrange("(f p) n -> p f n", p=P)

    def parts(f):
        c = slice(P * f, P * f + P)
        return (wg_h[:, :, c], wg_l[:, :, c]), (wu_h[:, :, c], wu_l[:, :, c]), (wd_h[:, f, :], wd_l[:, f, :])

    def staged_view(f, j):
        raw = stage[:, f % 2, j, :]
        return raw if j == 2 else raw.rearrange("p (k c) -> p k c", k=DK)

    with nc.Block() as block:
        @block.sync
        def _(sp):
            sp.dma_start(xs[:], x_v[0]).then_inc(x_landed, 16)
            for f in range(FK):
                if f >= 2:
                    sp.wait_ge(w_lo, 3 * (f - 1))
                srcs = (wg_v[:, :, P * f:P * f + P], wu_v[:, :, P * f:P * f + P], wd_v[:, f, :])
                for j in range(3):
                    sp.dma_start(staged_view(f, j), srcs[j]).then_inc(w_staged[f % 2][j], 16)
            with sp.Fori(0, NBLK - 1) as s:
                sp.wait_ge(y_done, s * ST + ST)
                sp.dma_start(o_v[bass.ds(s, 1)].rearrange("a p t d -> (a p) t d"), xs[:]).then_inc(stored, 16)
                sp.wait_ge(stored, s * 16 + 16)
                sp.dma_start(xs[:], x_v[bass.ds(s + 1, 1)].rearrange("a p t d -> (a p) t d"))\
                    .then_inc(x_landed, 16)
            sp.wait_ge(y_done, NBLK * ST)
            sp.dma_start(o_v[NBLK - 1], xs[:]).then_inc(stored, 16)
            sp.wait_ge(stored, NBLK * 16)

        @block.gpsimd
        def _(pool):
            with pool.Fori(0, NBLK) as s:
                pool.wait_ge(ve_done, s + 1)
                nc.gpsimd.tensor_tensor(rstd[:], ve[:], mhalf[:, 0:ST], ALU.pow).then_inc(rstd_done, 1)

        def act_block(act, s, load):
            def weights_hi(f):
                for j in range(3):
                    act.wait_ge(w_staged[f % 2][j], 16 * (f // 2) + 16)
                    nc.scalar.copy(parts(f)[j][0], staged_view(f, j)).then_inc(w_hi, 1)

            if load:
                weights_hi(0)
                weights_hi(1)
            for t in range(ST):
                act.wait_ge(xt_ready, s * ST + t + 1)
                nc.scalar.copy(xt_h[:, :, P * t:P * t + P],
                               score[:, t % 2, :].rearrange("p (k c) -> p k c", k=DK)).then_inc(xt_hi, 1)
            for f in range(FK):
                act.wait_ge(gu_ready, s * FK + f + 1)
                if f >= 2:
                    act.wait_ge(hid_done, s * FK + f - 1)
                nc.scalar.activation(gate[:, f % 2, :], score[:, 2 * (f % 2), :], ACT.Silu, scale=WSCALE)\
                    .then_inc(gate_done, 1)
                act.wait_ge(hid_done, s * FK + f + 1)
                if f >= 2:
                    act.wait_ge(down_done, s * FK + f - 1)
                nc.scalar.copy(hid_h[:, f % 2, :], hid[:]).then_inc(hidh_done, 1)
                if load and f + 2 < FK:
                    weights_hi(f + 2)

        @block.scalar
        def _(act):
            act_block(act, 0, True)
            with act.Fori(1, NBLK) as s:
                act_block(act, s, False)

        def dve_block(dve, s, load):
            V = nc.vector

            def weights_lo(f):
                for j in range(3):
                    hi, lo = parts(f)[j]
                    dve.wait_ge(w_hi, 3 * f + j + 1)
                    V.tensor_tensor(lo, staged_view(f, j), hi.bitcast(F32), ALU.subtract).then_inc(w_lo, 1)

            dve.wait_ge(x_landed, s * 16 + 16)
            for t in range(ST):
                V.bn_stats(stats[:, t, :], xs[:, t, :]).then_inc(st_done, 1)
            dve.wait_ge(st_done, s * ST + ST)
            V.memset(wait_pad[:, 0:1], 0.0)
            for t in range(ST):
                V.bn_aggr(mv[:, t, :], stats[:, t, :]).then_inc(ag_done, 1)
            dve.wait_ge(ag_done, s * ST + ST)
            V.tensor_scalar(ve[:], mv[:, :, 1], LN_EPS, None, ALU.add).then_inc(ve_done, 1)
            dve.wait_ge(rstd_done, s + 1)
            if load:
                weights_lo(0)
                weights_lo(1)

            def norm(t):
                if t >= 2:
                    dve.wait_ge(xt_ready, s * ST + t - 1)
                V.tensor_scalar(xn[:, t % 2, :], xs[:, t, :], mv[:, t, 0:1], rstd[:, t:t + 1],
                                ALU.subtract, ALU.mult).then_inc(xn_done, 1)

            norm(0)
            norm(1)
            for t in range(ST):
                if t + 2 < ST:
                    norm(t + 2)
                dve.wait_ge(xt_hi, s * ST + t + 1)
                V.tensor_tensor(xt_l[:, :, P * t:P * t + P],
                                score[:, t % 2, :].rearrange("p (k c) -> p k c", k=DK),
                                xt_h[:, :, P * t:P * t + P].bitcast(F32), ALU.subtract).then_inc(xt_lo, 1)
            for f in range(FK):
                dve.wait_ge(gate_done, s * FK + f + 1)
                if f >= 1:
                    dve.wait_ge(hidl_done, s * FK + f)
                V.scalar_tensor_tensor(hid[:], score[:, 2 * (f % 2) + 1, :], WSCALE, gate[:, f % 2, :],
                                       ALU.mult, ALU.mult).then_inc(hid_done, 1)
                dve.wait_ge(hidh_done, s * FK + f + 1)
                V.tensor_tensor(hid_l[:, f % 2, :], hid[:], hid_h[:, f % 2, :].bitcast(F32), ALU.subtract)\
                    .then_inc(hidl_done, 1)
                if load and f + 2 < FK:
                    weights_lo(f + 2)
            for t in range(ST):
                dve.wait_ge(down_done, s * FK + FK)
                V.scalar_tensor_tensor(xs[:, t, :], work[:, t, :], WSCALE, xs[:, t, :], ALU.mult, ALU.add)\
                    .then_inc(y_done, 1)

        @block.vector
        def _(dve):
            dve_block(dve, 0, True)
            with dve.Fori(1, NBLK) as s:
                dve_block(dve, s, False)

        def pe_block(pe, s, load):
            PE = nc.tensor
            for t in range(ST):
                pe.wait_ge(xn_done, s * ST + t + 1)
                if t >= 2:
                    pe.wait_ge(xt_lo, s * ST + t - 1)
                elif not load:
                    pe.wait_ge(hid_done, s * FK)
                for k in range(DK):
                    last = PE.transpose(score[:, t % 2, P * k:P * k + P], xn[:, t % 2, P * k:P * k + P], ident[:])
                last.then_inc(xt_ready, 1)
            pe.wait_ge(xt_lo, s * ST + ST)

            def up(f):
                if load:
                    pe.wait_ge(w_lo, 3 * f + 3)
                if f >= 2:
                    pe.wait_ge(hid_done, s * FK + f - 1)
                (g_h, g_l), (u_h, u_l), _ = parts(f)
                for bank, (w_h, w_l) in enumerate(((g_h, g_l), (u_h, u_l))):
                    for k in range(DK):
                        last = three(PE, score[:, 2 * (f % 2) + bank, :], w_h[:, k, :], w_l[:, k, :],
                                     xt_h[:, k, :], xt_l[:, k, :], k == 0, k == DK - 1)
                last.then_inc(gu_ready, 1)

            def down(f):
                pe.wait_ge(hidl_done, s * FK + f + 1)
                if f == 0 and not load:
                    pe.wait_ge(y_done, s * ST)
                for t in range(ST):
                    last = three(PE, work[:, t, :], hid_h[:, f % 2, P * t:P * t + P],
                                 hid_l[:, f % 2, P * t:P * t + P], wd_h[:, f, :], wd_l[:, f, :],
                                 f == 0, f == FK - 1)
                last.then_inc(down_done, 1)
                return last

            up(0)
            for f in range(1, FK):
                up(f)
                down(f - 1)
            down(FK - 1)

        @block.tensor
        def _(pe):
            pe_block(pe, 0, True)
            with pe.Fori(1, NBLK) as s:
                pe_block(pe, s, False)


_OUT_SHAPE = (2, 1024, 512)


def kernel(**inputs):
    import numpy as np
    import concourse.bacc as bacc
    from concourse.bass_utils import run_bass_kernel_spmd

    def arr(name):
        return np.asarray(inputs[name])

    x = arr("x").reshape(2, 512, 2, 512).transpose(0, 2, 1, 3).reshape(2048, 512)
    laid = {
        "x": x,
        "ctx_n": arr("ctx_1024"),
        "ctx_t": arr("ctx_1024").transpose(0, 2, 1),
        "wqkv_t": arr("L0_attn_qkv_w").T,
        "qkv_b": arr("L0_attn_qkv_b"),
        "wo_t": arr("L0_attn_out_w").T,
        "out_b": arr("L0_attn_out_b"),
        "wq_t": arr("L0_xattn_Wq").T,
        "bq": arr("L0_xattn_bq"),
        "wk_t": arr("L0_xattn_Wk").T,
        "bk": arr("L0_xattn_bk"),
        "wv": arr("L0_xattn_Wv"),
        "bv": arr("L0_xattn_bv"),
        "wg_t": arr("L0_ffn_w_gate").T,
        "wu_t": arr("L0_ffn_w_up").T,
        "wd_t": arr("L0_ffn_w_down").T,
    }
    nc = bacc.Bacc("TRN2", target_bir_lowering=False, num_devices=1)
    arrays, args = {}, []
    for name, a in laid.items():
        a = np.ascontiguousarray(a)
        arrays[f"in_{name}"] = a
        args.append(nc.dram_tensor(f"in_{name}", a.shape, mybir.dt.from_np(a.dtype), kind="ExternalInput").ap())
    args.append(nc.dram_tensor("out_y", (2048, 512), F32, kind="ExternalOutput").ap())
    decoder_layer(nc, *args)
    r = run_bass_kernel_spmd(nc, [arrays], core_ids=[0])
    y = r.results[0]["out_y"].reshape(2, 2, 512, 512).transpose(0, 2, 1, 3).reshape(_OUT_SHAPE)
    return np.ascontiguousarray(y)
```

```python
from contextlib import ExitStack

import concourse.bass as bass
from concourse import mybir

F32 = mybir.dt.float32
F32R = mybir.dt.float32r
I32 = mybir.dt.int32
ALU = mybir.AluOpType
ACT = mybir.ActivationFunctionType
AX = mybir.AxisListType

P = 128
NB = 2
T = 2048
D = 512
DK = D // P
SEQ = 512
ST = SEQ // P
NT = T // P
HG = 4
HPG = 4
DH = 32
H = HG * HPG
HALO = 8
WIN = P + 2 * HALO
CTX = 2048
CK = CTX // P
BT = T // NB // P
FH = 1536
FK = FH // P
NBLK = T // SEQ
LN_EPS = 1e-5
NORM_EPS = 1e-6
WSCALE = 1.0 / 127.0


def three(pe, out, hi_s, lo_s, hi_m, lo_m, first, last):
    pe.matmul(out, hi_s, hi_m, start=first, stop=False)
    pe.matmul(out, hi_s, lo_m, start=False, stop=False)
    return pe.matmul(out, lo_s, hi_m, start=False, stop=last)


def decoder_layer(nc, x, ctx_n, wqkv_t, qkv_b, wo_t, out_b, wq_t, bq, wk_t, bk, wv, bv,
                  wg_t, wu_t, wd_t, out):
    x1_dram = nc.dram_tensor("x1_scratch", [T, D], F32, kind="Internal").ap()
    x2_dram = nc.dram_tensor("x2_scratch", [T, D], F32, kind="Internal").ap()
    qp_dram = nc.dram_tensor("qp_scratch", [NT, P, D], F32, kind="Internal").ap()
    with ExitStack() as ctx:
        def sb(scope, name, shape, dt=F32):
            return scope.enter_context(nc.sbuf_tensor(name, shape, dt))

        def sem(name):
            return ctx.enter_context(nc.semaphore(name))

        score = ctx.enter_context(nc.psum_tensor("score", [P, 4, 512], F32))
        work = ctx.enter_context(nc.psum_tensor("work", [P, 4, 512], F32))
        wait_pad = sb(ctx, "wait_pad", [P, 2 + 2 * ST])
        ident = sb(ctx, "ident", [P, P])
        mhalf = sb(ctx, "mhalf", [P, ST])
        q_const = sb(ctx, "q_const", [P, NT])

        with ExitStack() as attn:
            attention_phase(nc, ctx, attn, sb, sem, score, work, ident, mhalf, wait_pad, q_const,
                            x, wqkv_t, qkv_b, wo_t, out_b, wq_t, bq, wk_t, bk, x1_dram, qp_dram)
        with ExitStack() as cross:
            cross_phase(nc, cross, sb, sem, score, work, ident, q_const,
                        ctx_n, wv, bv, x1_dram, qp_dram, x2_dram)
        with ExitStack() as ffn:
            ffn_phase(nc, ffn, sb, sem, score, work, ident, mhalf, wait_pad, wg_t, wu_t, wd_t, x2_dram, out)


def attention_phase(nc, ctx, scope, sb, sem, score, work, ident, mhalf, wait_pad, q_const,
                    x, wqkv_t, qkv_b, wo_t, out_b, wq_t, bq, wk_t, bk, x1_dram, qp_dram):
    GW = 3 * P
    wqkv_h = sb(scope, "wqkv_h", [P, DK, HG, GW], F32R)
    wqkv_l = sb(scope, "wqkv_l", [P, DK, HG, GW], F32R)
    wo_h = sb(scope, "wo_h", [P, DK, D], F32R)
    wo_l = sb(scope, "wo_l", [P, DK, D], F32R)
    wp_h = sb(scope, "wp_h", [P, DK, D], F32R)
    wp_l = sb(scope, "wp_l", [P, DK, D], F32R)
    qkb_row = sb(scope, "qkb_row", [P, HG, 2 * P])
    ob_row = sb(scope, "ob_row", [P, D])
    wqb_row = sb(scope, "wqb_row", [P, D])
    bqp = sb(scope, "bqp", [P, DK])
    bqbk = sb(scope, "bqbk", [P, 1])
    ones = sb(scope, "ones", [P, DH])
    band = sb(scope, "band", [P, WIN])

    with ExitStack() as st:
        raw = sb(st, "w_raw", [P, DK, HG * GW])
        raw_o = sb(st, "wo_raw", [P, DK, D])
        raw_q = sb(st, "wq_raw", [P, DK, D])
        raw_k = sb(st, "wk_raw", [P, DK, D])
        q_h = sb(st, "wq_h", [P, DK, D], F32R)
        q_l = sb(st, "wq_l", [P, DK, D], F32R)
        cols = sb(st, "cols", [P, 3, DK])
        wide = sb(st, "wide", [P, 2, DK, P])
        k_h = sb(st, "wk_h", [P, DK, D], F32R)
        k_l = sb(st, "wk_l", [P, DK, D], F32R)
        w_landed = [sem(f"w_landed{i}") for i in range(5)]
        rows_landed = sem("rows_landed")
        set_hi = sem("set_hi")
        set_lo = sem("set_lo")
        wide_ready = sem("wide_ready")
        consts = sem("consts")
        bias_ready = sem("bias_ready")
        bias_read = sem("bias_read")
        prod_ready = sem("prod_ready")
        prod_hi = sem("prod_hi")
        prod_lo = sem("prod_lo")
        qkv_b_v = qkv_b.rearrange("(g n) -> g n", g=HG)
        with nc.Block() as block:
            @block.sync
            def _(sp):
                sp.dma_start(raw_q[:], wq_t.rearrange("(k p) n -> p k n", p=P)).then_inc(w_landed[0], 16)
                sp.dma_start(raw_k[:], wk_t.rearrange("(k p) n -> p k n", p=P)).then_inc(w_landed[1], 16)
                sp.dma_start(cols[:, 0, :], bq.rearrange("(k p) -> p k", p=P),
                             allow_slow_non_contiguous=True).then_inc(w_landed[4], 16)
                sp.dma_start(cols[:, 1, :], bk.rearrange("(k p) -> p k", p=P),
                             allow_slow_non_contiguous=True).then_inc(w_landed[4], 16)
                sp.dma_start(cols[:, 2, :], qkv_b_v[:, 2 * P:3 * P].rearrange("g p -> p g"),
                             allow_slow_non_contiguous=True).then_inc(w_landed[4], 16)
                sp.dma_start(raw_o[:], wo_t.rearrange("(k p) n -> p k n", p=P)).then_inc(w_landed[2], 16)
                sp.dma_start(raw[:], wqkv_t.rearrange("(k p) n -> p k n", p=P)).then_inc(w_landed[3], 16)
                sp.dma_start(qkb_row[:], qkv_b_v[:, 0:2 * P].partition_broadcast(P)).then_inc(rows_landed, 16)
                sp.dma_start(ob_row[:], out_b.partition_broadcast(P)).then_inc(rows_landed, 16)
                sp.wait_ge(rows_landed, 32)

            @block.gpsimd
            def _(pool):
                nc.gpsimd.memset(ident[:], 0.0).then_inc(consts, 1)
                nc.gpsimd.memset(band[:], 1.0).then_inc(consts, 1)
                nc.gpsimd.memset(mhalf[:], -0.5).then_inc(consts, 1)
                nc.gpsimd.memset(ones[:], 1.0).then_inc(consts, 1)
                pool.wait_ge(consts, 4)
                nc.gpsimd.affine_select(out=ident[:], in_=ident[:], compare_op=ALU.not_equal, fill=1.0,
                                        base=0, pattern=[[-1, P]], channel_multiplier=1).then_inc(consts, 1)
                nc.gpsimd.affine_select(out=band[:], in_=band[:], compare_op=ALU.is_ge, fill=0.0,
                                        base=0, pattern=[[1, WIN]], channel_multiplier=-1).then_inc(consts, 1)
                pool.wait_ge(consts, 6)
                nc.gpsimd.affine_select(out=band[:], in_=band[:], compare_op=ALU.is_ge, fill=0.0,
                                        base=2 * HALO, pattern=[[-1, WIN]], channel_multiplier=1)\
                    .then_inc(consts, 1)

            sets = ((raw_q, q_h, q_l, 0), (raw_k, k_h, k_l, 1), (raw_o, wo_h, wo_l, 2),
                    (raw, wqkv_h, wqkv_l, 3))

            @block.scalar
            def _(act):
                for src, hi, lo, n in sets[:2]:
                    act.wait_ge(w_landed[n], 16)
                    nc.scalar.copy(hi[:], src[:]).then_inc(set_hi, 1)
                act.wait_ge(w_landed[2], 16)
                nc.scalar.copy(wo_h[:], raw_o[:]).then_inc(set_hi, 1)
                act.wait_ge(w_landed[3], 16)
                for k in range(DK):
                    nc.scalar.copy(wqkv_h[:, k].rearrange("p g n -> p (g n)"), raw[:, k, :]).then_inc(set_hi, 1)
                for m in range(DK):
                    act.wait_ge(prod_ready, m + 1)
                    nc.scalar.copy(wp_h[:, m, :], score[:, m, :]).then_inc(prod_hi, 1)

            @block.vector
            def _(dve):
                dve.wait_ge(w_landed[4], 48)
                nc.vector.tensor_copy(wide[:], cols[:, 1:3, :].unsqueeze(3).to_broadcast([P, 2, DK, P]))\
                    .then_inc(wide_ready, 1)
                for n, (src, hi, lo, _) in enumerate(sets[:3]):
                    dve.wait_ge(set_hi, n + 1)
                    nc.vector.tensor_tensor(lo[:], src[:], hi[:].bitcast(F32), ALU.subtract).then_inc(set_lo, 1)
                for k in range(DK):
                    dve.wait_ge(set_hi, 4 + k)
                    nc.vector.tensor_tensor(wqkv_l[:, k].rearrange("p g n -> p (g n)"), raw[:, k, :],
                                            wqkv_h[:, k].rearrange("p g n -> p (g n)").bitcast(F32),
                                            ALU.subtract).then_inc(set_lo, 1)
                for m in range(DK):
                    dve.wait_ge(prod_hi, m + 1)
                    nc.vector.tensor_tensor(wp_l[:, m, :], score[:, m, :], wp_h[:, m, :].bitcast(F32),
                                            ALU.subtract).then_inc(prod_lo, 1)
                dve.wait_ge(bias_ready, 1)
                dve.wait_ge(rows_landed, 32)
                nc.vector.tensor_copy(wqb_row[:], work[:, 0, :]).then_inc(bias_read, 1)
                nc.vector.tensor_copy(bqp[:], work[:, 1, 0:DK]).then_inc(bias_read, 1)
                nc.vector.tensor_copy(bqbk[:], work[:, 2, 0:1]).then_inc(bias_read, 1)
                nc.vector.tensor_tensor(ob_row[:], work[:, 3, :], ob_row[:], ALU.add).then_inc(bias_read, 1)

            @block.tensor
            def _(pe):
                pe.wait_ge(wide_ready, 1)
                pe.wait_ge(w_landed[0], 16)
                pe.wait_ge(w_landed[1], 16)
                for e in range(DK):
                    nc.tensor.matmul(work[:, 0, :], wide[:, 0, e, :], raw_q[:, e, :],
                                     start=e == 0, stop=e == DK - 1)
                pe.wait_ge(set_lo, 2)
                for m in range(DK):
                    for e in range(DK):
                        last = three(nc.tensor, score[:, m, :], q_h[:, e, P * m:P * m + P],
                                     q_l[:, e, P * m:P * m + P], k_h[:, e, :], k_l[:, e, :],
                                     e == 0, e == DK - 1)
                    last.then_inc(prod_ready, 1)
                for e in range(DK):
                    nc.tensor.matmul(work[:, 2, 0:1], wide[:, 0, e, :], cols[:, 0, e:e + 1],
                                     start=e == 0, stop=e == DK - 1)
                for m in range(DK):
                    for e in range(DK):
                        nc.tensor.matmul(work[:, 1, m:m + 1], raw_k[:, e, P * m:P * m + P],
                                         cols[:, 0, e:e + 1], start=e == 0, stop=e == DK - 1)
                pe.wait_ge(w_landed[2], 16)
                for e in range(DK):
                    last = nc.tensor.matmul(work[:, 3, :], wide[:, 1, e, :], raw_o[:, e, :],
                                            start=e == 0, stop=e == DK - 1)
                last.then_inc(bias_ready, 1)

    xs = sb(scope, "xs", [P, 2, ST, D])
    xn = sb(scope, "xn", [P, 2, D])
    xt_h = sb(scope, "xt_h", [P, DK, SEQ], F32R)
    xt_l = sb(scope, "xt_l", [P, DK, SEQ], F32R)
    ot_h = sb(scope, "ot_h", [P, DK, SEQ], F32R)
    ot_l = sb(scope, "ot_l", [P, DK, SEQ], F32R)
    qk = sb(scope, "qk", [P, 2, ST, 2 * P])
    v = sb(scope, "v", [P, HG, ST, P])
    qbd_h = sb(scope, "qbd_h", [P, 2, HPG, SEQ], F32R)
    qbd_l = sb(scope, "qbd_l", [P, 2, HPG, SEQ], F32R)
    kt_h = sb(scope, "kt_h", [P, 2, SEQ], F32R)
    kt_l = sb(scope, "kt_l", [P, 2, SEQ], F32R)
    probs = sb(scope, "probs", [P, 2, HPG, WIN])
    pair = sb(scope, "pair", [P, 2, SEQ])
    stats = sb(scope, "stats", [P, ST, 6])
    mv = sb(scope, "mv", [P, ST, 2])
    ve = sb(scope, "ve", [P, ST])
    rstd = sb(scope, "rstd", [P, ST])
    stats2 = sb(scope, "stats2", [P, ST, 6])
    mv2 = sb(scope, "mv2", [P, ST, 2])
    ve2 = sb(scope, "ve2", [P, ST])
    rstd2 = sb(scope, "rstd2", [P, ST])
    NH = ST * 2 * HPG
    ss = sb(scope, "ss", [P, NH])
    ry = sb(scope, "ry", [P, NH])
    ru = sb(scope, "ru", [P, NH])
    rnrm = sb(scope, "rnrm", [P, 2, NH])
    rsum, o_sc = pair[:, 0, :], pair[:, 1, :]

    def unit_tile(g, i, last):
        if g < 2:
            return 0, g + 2, i
        if g == 2 and not last:
            return 1, 0, i
        if g == 3 and not last and i != 1:
            return 1, 1, (0, None, 1, 2)[i]
        return None

    def step_uses(g, last):
        uses = []
        for i in range(ST):
            if g == 2 and not last and i < 2:
                uses.append(("xt", i + 1))
            if unit_tile(g, i, last):
                uses.append(("qkv",) + unit_tile(g, i, last))
            if g == 2 and not last and i == 1:
                uses.append(("xt", 3))
            if i == 1 and (g < HG - 1 or not last):
                uses += [("kt", g + 1), ("qt", g + 1)]
            if g == 1 and not last and i == 3:
                uses.append(("xt", 0))
        return uses

    tail = ["q3", "o0", "o1", "o2", "x0", "o3", "x1", "x2", "x3"]

    def all_uses(last):
        uses = [u for g in range(HG) for u in step_uses(g, last)]
        for what in tail:
            t = int(what[1])
            if what[0] == "q" and not last:
                uses.append(("qkv", 1, 1, t))
            if what[0] == "o":
                uses.append(("op", t))
            if what[0] == "x":
                uses.append(("x2t", t))
        return uses + [("qp", m) for m in range(DK)]

    pro_uses = [("xt", t) for t in range(ST)] + [("qkv", 1, g, t) for g in range(2) for t in range(ST)]
    pro_uses += [("kt", HG), ("qt", HG)]
    PRO = len(pro_uses)
    pro = {u: n for n, u in enumerate(pro_uses)}
    NU = len(all_uses(False))
    use = [{u: PRO + n for n, u in enumerate(all_uses(last))} for last in (False, True)]
    assert PRO % 2 == 0 and NU % 2 == 0

    class Seq:
        def __init__(self, s, last=False, lead=False):
            self.s, self.last, self.lead = s, last, lead
            self.use = pro if lead else use[last]

        def nth(self, key):
            return self.use[key] if self.lead else self.s * NU + self.use[key]

        def bank(self, key):
            return work[:, self.use[key] % 2, :]

        def filled(self, key):
            return self.nth(key) + 1

        def read(self, key):
            return self.nth(key) + 3

        def scaled(self, g):
            return self.s * (HG + 1) + g + (g == HG)

        def group(self, g):
            return g - HG if self.lead else self.s * HG + g

    x_landed = sem("x_landed")
    filled = sem("work_filled")
    released = sem("work_released")
    bd_zero = sem("bd_zero")
    st_done = sem("st_done")
    ag_done = sem("ag_done")
    ve_done = sem("ve_done")
    rstd_done = sem("rstd_done")
    xn_done = sem("xn_done")
    xb_done = sem("xb_done")
    xt_hi = sem("xt_hi")
    v_done = sem("v_done")
    sq_done = sem("sq_done")
    ss_done = sem("ss_done")
    nw_done = sem("newton_done")
    rn_done = sem("rnorm_done")
    qk_done = sem("qk_done")
    kq_hi = sem("kq_hi")
    len_done = sem("len_done")
    s_ready = sem("s_ready")
    exp_done = sem("exp_done")
    p_ready = sem("p_ready")
    pv_done = sem("pv_done")
    o_copied = sem("o_copied")
    rs_done = sem("rs_done")
    os_done = sem("os_done")
    ot_hi = sem("ot_hi")
    ot_lo = sem("ot_lo")
    st2_done = sem("st2_done")
    ag2_done = sem("ag2_done")
    ve2_done = sem("ve2_done")
    rstd2_done = sem("rstd2_done")
    xn2_done = sem("xn2_done")
    c_done = sem("c_done")
    xt2_hi = sem("xt2_hi")
    cb_done = sem("cb_done")
    x1_stored = sem("x1_stored")
    qp_stored = sem("qp_stored")

    def window(i):
        lo, hi = max(0, P * i - HALO), min(SEQ, P * i + P + HALO)
        return lo, hi - lo, lo - (P * i - HALO)

    x_v = x.rearrange("(s t p) d -> s p t d", t=ST, p=P)
    x1_v = x1_dram.rearrange("(s t p) d -> s p t d", t=ST, p=P)
    qp_v = qp_dram.rearrange("(s t) p n -> s p t n", t=ST)
    NS = 2 * NB
    NCHAIN = 11

    def run(eng, lead_in, body):
        lead_in(Seq(-1, lead=True))
        with eng.Fori(0, NS - 1) as s:
            body(Seq(s))
        body(Seq(NS - 1, last=True))

    def xs_tile(s, t):
        if isinstance(s, int):
            return xs[:, s % 2, t, :]
        return xs[:].rearrange("p a t d -> p (a t) d")[:, bass.ds((s % 2) * ST + t, 1), :]\
            .rearrange("p a d -> p (a d)")

    def pieces(g):
        half = SEQ // 2
        return (slice(0, half), slice(half, SEQ)) if g == HG - 1 else (slice(0, SEQ),)

    with nc.Block() as block:
        @block.sync
        def _(sp):
            for s in range(2):
                sp.dma_start(xs[:, s], x_v[s]).then_inc(x_landed, 16)
                sp.wait_ge(x_landed, 16 * s + 16)
            for s in range(NS):
                q = Seq(s, last=s == NS - 1)
                sp.wait_ge(released, q.read(("op", ST - 1)))
                sp.dma_start(x1_v[s], xs[:, s % 2]).then_inc(x1_stored, 16)
                sp.wait_ge(released, q.read(("qp", DK - 1)))
                sp.dma_start(qp_v[s], xs[:, s % 2]).then_inc(qp_stored, 16)
                if s + 2 < NS:
                    sp.wait_ge(qp_stored, s * 16 + 16)
                    sp.wait_ge(x_landed, 16 * (s + 2))
                    sp.dma_start(xs[:, s % 2], x_v[s + 2]).then_inc(x_landed, 16)
            sp.wait_ge(x1_stored, 16 * NS)
            sp.wait_ge(qp_stored, 16 * NS)

        @block.gpsimd
        def _(pool):
            def root(n):
                pool.wait_ge(ve_done, n + 1)
                nc.gpsimd.tensor_tensor(rstd[:], ve[:], mhalf[:, 0:ST], ALU.pow).then_inc(rstd_done, 1)

            def scale_units(q, g):
                k = q.group(g)
                pool.wait_ge(rn_done, k + 1)
                q3 = qk[:, g % 2].rearrange("p t (h d) -> p (t h) d", d=DH)
                nc.gpsimd.tensor_tensor(q3, q3, rnrm[:, g % 2, :].unsqueeze(2).to_broadcast([P, NH, DH]),
                                        ALU.mult).then_inc(qk_done, 1)

            def mask(q, n):
                lo, w, c0 = window(n % ST)
                pool.wait_ge(exp_done, q.group(0) * ST + n + 1 if not q.lead else n - HG * ST + 1)
                nc.gpsimd.tensor_tensor(probs[:, n % 2, :, 0:w], probs[:, n % 2, :, 0:w],
                                        band[:, c0:c0 + w].unsqueeze(1).to_broadcast([P, HPG, w]),
                                        ALU.mult).then_inc(p_ready, 1)

            def out_lo(q, g):
                for n, c in enumerate(pieces(g)):
                    pool.wait_ge(ot_hi, q.scaled(g) + n + 1)
                    nc.gpsimd.tensor_tensor(ot_l[:, g, c], o_sc[:, c], ot_h[:, g, c].bitcast(F32),
                                            ALU.subtract).then_inc(ot_lo, 1)

            def lead_in(q):
                nc.gpsimd.memset(qbd_h[:].bitcast(F32), 0.0).then_inc(bd_zero, 1)
                nc.gpsimd.memset(qbd_l[:].bitcast(F32), 0.0).then_inc(bd_zero, 1)
                root(0)
                scale_units(q, HG)
                scale_units(q, HG + 1)
                mask(q, HG * ST)
                mask(q, HG * ST + 1)

            def body(q):
                for g in range(HG):
                    for i in range(ST):
                        n = ST * g + i
                        if g == 0:
                            if i == 0:
                                pool.wait_ge(xn_done, (q.s + 1) * ST)
                            xt_ = xs_tile(q.s, i)
                            nc.gpsimd.tensor_tensor(xt_, xt_, ob_row[:], ALU.add).then_inc(xb_done, 1)
                        if i == 1 and g:
                            pool.wait_ge(rs_done, q.scaled(g))
                            nc.gpsimd.tensor_tensor(o_sc, o_sc, rsum, ALU.mult).then_inc(os_done, 1)
                        if i == 2 and g:
                            out_lo(q, g - 1)
                        if g == 1 and i == 3 and not q.last:
                            root(q.s + 1)
                        if n + 2 < HG * ST or not q.last:
                            mask(q, n + 2)
                    if g < 2:
                        scale_units(q, g + 2)
                    elif g == 2 and not q.last:
                        scale_units(q, HG)
                out_lo(q, HG - 1)
                for t in range(ST):
                    pool.wait_ge(ve2_done, q.s * ST + t + 1)
                    nc.gpsimd.tensor_tensor(rstd2[:, t:t + 1], ve2[:, t:t + 1], mhalf[:, 0:1], ALU.pow)\
                        .then_inc(rstd2_done, 1)
                if not q.last:
                    scale_units(q, HG + 1)

            run(pool, lead_in, body)

        @block.scalar
        def _(act):
            def hi_tile(q, kind, t, dst, done):
                act.wait_ge(filled, q.filled((kind, t)))
                nc.scalar.copy(dst[:, :, P * t:P * t + P],
                               q.bank((kind, t)).rearrange("p (k c) -> p k c", k=DK)).then_inc(done, 1)

            def v_tile(q, d, g, t):
                key = ("qkv", d, g, t)
                act.wait_ge(filled, q.filled(key))
                nc.scalar.copy(v[:, g, t, :], q.bank(key)[:, 2 * P:3 * P]).then_inc(v_done, 1)

            def squares(q, d, g):
                act.wait_ge(released, q.read(("qkv", d, g, ST - 1)))
                nc.scalar.activation(pair[:].rearrange("p a n -> p (a n)"),
                                     qk[:, g % 2].rearrange("p t n -> p (t n)"), ACT.Square).then_inc(sq_done, 1)

            def key_hi(q, g):
                act.wait_ge(filled, q.filled(("kt", g)))
                nc.scalar.copy(kt_h[:, g % 2, :], q.bank(("kt", g))).then_inc(kq_hi, 1)

            def query_hi(q, g, h):
                act.wait_ge(filled, q.filled(("qt", g)))
                r = slice(DH * h, DH * h + DH)
                nc.scalar.copy(qbd_h[r, g % 2, h, :], q.bank(("qt", g))[r, :]).then_inc(kq_hi, 1)

            def exp(q, n, first=False):
                lo, w, c0 = window(n % ST)
                unit = n - HG * ST if q.lead else q.group(0) * ST + n
                act.wait_ge(s_ready, unit + 1)
                if not first:
                    act.wait_ge(pv_done, unit - 1)
                b0 = 2 * (n % 2)
                nc.scalar.activation(
                    probs[:, n % 2].rearrange("p (a h) w -> p a h w", a=2)[:, :, :, 0:w],
                    score[:, b0:b0 + 2, 0:2 * WIN].rearrange("p a (h w) -> p a h w", h=2)[:, :, :, 0:w],
                    ACT.Exp).then_inc(exp_done, 1)

            def copy_out(q, g):
                act.wait_ge(pv_done, q.group(g) * ST + ST)
                nc.scalar.copy(rsum, work[:, 3, :]).then_inc(o_copied, 1)
                nc.scalar.copy(o_sc, work[:, 2, :]).then_inc(o_copied, 1)

            def out_hi(q, g):
                for n, c in enumerate(pieces(g)):
                    act.wait_ge(os_done, q.scaled(g) + n + 1)
                    nc.scalar.copy(ot_h[:, g, c], o_sc[:, c]).then_inc(ot_hi, 1)

            def lead_in(q):
                for t in range(ST):
                    hi_tile(q, "xt", t, xt_h, xt_hi)
                for g in range(2):
                    for t in range(ST):
                        v_tile(q, 1, g, t)
                    if g == 1:
                        act.wait_ge(ss_done, 1)
                    squares(q, 1, g)
                act.wait_ge(bd_zero, 2)
                key_hi(q, HG)
                for h in range(HPG):
                    query_hi(q, HG, h)
                exp(q, HG * ST, True)
                exp(q, HG * ST + 1, True)

            def body(q):
                for g in range(HG):
                    for i in range(ST):
                        n = ST * g + i
                        if g == 2 and not q.last and i < 2:
                            hi_tile(q, "xt", i + 1, xt_h, xt_hi)
                        if unit_tile(g, i, q.last):
                            v_tile(q, *unit_tile(g, i, q.last))
                        if g == 2 and not q.last and i == 1:
                            hi_tile(q, "xt", 3, xt_h, xt_hi)
                        if i == 1 and (g < HG - 1 or not q.last):
                            key_hi(q, g + 1)
                            for h in range(HPG):
                                query_hi(q, g + 1, h)
                        if i == 1 and g:
                            out_hi(q, g - 1)
                        more = n + 2 < HG * ST or not q.last
                        if i == 3:
                            if g < 2 or (g == 2 and not q.last):
                                if g:
                                    act.wait_ge(ot_lo, q.scaled(g))
                                else:
                                    act.wait_ge(ss_done, q.group(0) + 2)
                                squares(q, int(g == 2), (g + 2) % HG)
                                if more:
                                    exp(q, n + 2)
                                act.wait_ge(ss_done, q.group(g) + 3)
                            else:
                                if more:
                                    exp(q, n + 2)
                                act.wait_ge(ot_lo, q.scaled(g))
                            copy_out(q, g)
                            if g == 1 and not q.last:
                                hi_tile(q, "xt", 0, xt_h, xt_hi)
                        elif more:
                            exp(q, n + 2)
                for what in tail:
                    t = int(what[1])
                    if what[0] == "q" and not q.last:
                        v_tile(q, 1, 1, t)
                    if what == "q3":
                        out_hi(q, HG - 1)
                    if what[0] == "x":
                        hi_tile(q, "x2t", t, ot_h, xt2_hi)
                if not q.last:
                    act.wait_ge(ot_lo, q.scaled(HG))
                    act.wait_ge(c_done, q.s * ST + ST)
                    squares(q, 1, 1)

            run(act, lead_in, body)

        @block.vector
        def _(dve):
            V = nc.vector

            def stats1(n, s):
                dve.wait_ge(x_landed, n * 16 + 16)
                V.memset(wait_pad[:, 1 + ST:2 + ST], 0.0)
                for t in range(ST):
                    V.bn_stats(stats[:, t, :], xs_tile(s, t)).then_inc(st_done, 1)
                dve.wait_ge(st_done, n * ST + ST)
                V.memset(wait_pad[:, 0:1], 0.0)
                for t in range(ST):
                    V.bn_aggr(mv[:, t, :], stats[:, t, :]).then_inc(ag_done, 1)
                dve.wait_ge(ag_done, n * ST + ST)
                V.tensor_scalar(ve[:], mv[:, :, 1], LN_EPS, None, ALU.add).then_inc(ve_done, 1)

            def norm1(q, n, s, t):
                if t == 0:
                    dve.wait_ge(rstd_done, n + 1)
                if t >= 2:
                    dve.wait_ge(filled, q.filled(("xt", t - 2)))
                V.tensor_scalar(xn[:, t % 2, :], xs_tile(s, t), mv[:, t, 0:1], rstd[:, t:t + 1],
                                ALU.subtract, ALU.mult).then_inc(xn_done, 1)

            def lo_tile(q, kind, n, t, hi, lo, hi_sem):
                dve.wait_ge(hi_sem, n * ST + t + 1)
                V.tensor_tensor(lo[:, :, P * t:P * t + P],
                                q.bank((kind, t)).rearrange("p (k c) -> p k c", k=DK),
                                hi[:, :, P * t:P * t + P].bitcast(F32), ALU.subtract).then_inc(released, 1)

            def qk_tile(q, d, g, t):
                key = ("qkv", d, g, t)
                tiles = (q.group(g) if not d else q.group(g + HG)) * ST if not q.lead else g * ST
                dve.wait_ge(v_done, tiles + t + 1)
                V.tensor_tensor(qk[:, g % 2, t, :], q.bank(key)[:, 0:2 * P], qkb_row[:, g, :], ALU.add)\
                    .then_inc(released, 1)

            def lengths(q, g, between=None):
                k = q.group(g)
                dve.wait_ge(sq_done, k + 1)
                V.tensor_reduce(ss[:], pair[:].rearrange("p a (h d) -> p (a h) d", d=DH), AX.X, ALU.add)\
                    .then_inc(ss_done, 1)
                if between:
                    between()
                dve.wait_ge(ss_done, k + 1)
                V.tensor_scalar(ru[:].bitcast(I32), ss[:].bitcast(I32), 1, None, ALU.logical_shift_right)\
                    .then_inc(nw_done, 1)
                dve.wait_ge(nw_done, k * NCHAIN + 1)
                V.tensor_scalar(ry[:].bitcast(I32), ru[:].bitcast(I32), -1.0, float(0x5F3759DF),
                                ALU.mult, ALU.add).then_inc(nw_done, 1)
                c = 2
                for _ in range(3):
                    dve.wait_ge(nw_done, k * NCHAIN + c)
                    V.scalar_tensor_tensor(ru[:], ry[:], -0.5, ss[:], ALU.mult, ALU.mult).then_inc(nw_done, 1)
                    dve.wait_ge(nw_done, k * NCHAIN + c + 1)
                    V.tensor_tensor(ru[:], ru[:], ry[:], ALU.mult).then_inc(nw_done, 1)
                    dve.wait_ge(nw_done, k * NCHAIN + c + 2)
                    V.scalar_tensor_tensor(ry[:], ru[:], 1.5, ry[:], ALU.add, ALU.mult).then_inc(nw_done, 1)
                    c += 3
                assert c == NCHAIN
                dve.wait_ge(nw_done, k * NCHAIN + c)
                V.tensor_tensor(ru[:], ss[:], ry[:], ALU.mult).then_inc(len_done, 1)
                dve.wait_ge(len_done, k * 2 + 1)
                V.tensor_scalar(ru[:], ru[:], NORM_EPS, None, ALU.add).then_inc(len_done, 1)
                dve.wait_ge(len_done, k * 2 + 2)
                V.reciprocal(rnrm[:, g % 2, :], ru[:]).then_inc(rn_done, 1)

            def key_query_lo(q, g):
                k = q.group(g)
                dve.wait_ge(kq_hi, k * 5 + 1)
                V.tensor_tensor(kt_l[:, g % 2, :], q.bank(("kt", g)), kt_h[:, g % 2, :].bitcast(F32),
                                ALU.subtract).then_inc(released, 1)
                for h in range(HPG):
                    dve.wait_ge(kq_hi, k * 5 + 2 + h)
                    r = slice(DH * h, DH * h + DH)
                    last = V.tensor_tensor(qbd_l[r, g % 2, h, :], q.bank(("qt", g))[r, :],
                                           qbd_h[r, g % 2, h, :].bitcast(F32), ALU.subtract)
                last.then_inc(released, 1)

            def out_scale(q, g):
                k = q.group(g)
                dve.wait_ge(o_copied, 2 * k + 2)
                for n, c in enumerate(pieces(g)):
                    V.reciprocal(rsum[:, c], rsum[:, c]).then_inc(rs_done, 1)
                    if g == HG - 1:
                        dve.wait_ge(rs_done, q.scaled(g) + n + 1)
                        V.tensor_tensor(o_sc[:, c], o_sc[:, c], rsum[:, c], ALU.mult).then_inc(os_done, 1)

            def residual(q, t):
                dve.wait_ge(filled, q.filled(("op", t)))
                if t == 0:
                    dve.wait_ge(xb_done, q.s * ST + ST)
                x_ = xs_tile(q.s, t)
                V.tensor_tensor(x_, q.bank(("op", t)), x_, ALU.add).then_inc(released, 1)
                dve.wait_ge(released, q.read(("op", t)))

            def stats2_of(q, t):
                k = q.s * ST + t + 1
                V.memset(wait_pad[:, 2 + ST + t:3 + ST + t], 0.0)
                V.bn_stats(stats2[:, t, :], xs_tile(q.s, t)).then_inc(st2_done, 1)
                dve.wait_ge(st2_done, k)
                V.memset(wait_pad[:, 1 + t:2 + t], 0.0)
                V.bn_aggr(mv2[:, t, :], stats2[:, t, :]).then_inc(ag2_done, 1)
                dve.wait_ge(ag2_done, k)
                V.tensor_scalar(ve2[:, t:t + 1], mv2[:, t, 1:2], LN_EPS, None, ALU.add).then_inc(ve2_done, 1)

            def norm2(q, t):
                k = q.s * ST + t + 1
                dve.wait_ge(rstd2_done, k)
                if t >= 2:
                    dve.wait_ge(filled, q.filled(("x2t", t - 2)))
                V.tensor_scalar(xn[:, t % 2, :], xs_tile(q.s, t), mv2[:, t, 0:1], rstd2[:, t:t + 1],
                                ALU.subtract, ALU.mult).then_inc(xn2_done, 1)
                dve.wait_ge(xn2_done, k)
                V.scalar_tensor_tensor(rsum, xn[:, t % 2, :], 1.0, wqb_row[:], ALU.mult, ALU.mult,
                                       accum_out=ve2[:, t:t + 1]).then_inc(c_done, 1)
                dve.wait_ge(c_done, k)

            def lead_in(q):
                V.memset(stats[:, 0, :], 0.0).then_inc(released, 1)
                V.memset(stats[:, 1, :], 0.0).then_inc(released, 1)
                dve.wait_ge(released, 2)
                stats1(0, 0)
                norm1(q, 0, 0, 0)
                norm1(q, 0, 0, 1)
                for t in range(ST):
                    if t + 2 < ST:
                        norm1(q, 0, 0, t + 2)
                    lo_tile(q, "xt", 0, t, xt_h, xt_l, xt_hi)
                for g in range(2):
                    for t in range(ST):
                        qk_tile(q, 1, g, t)
                    lengths(q, HG + g)
                dve.wait_ge(bd_zero, 2)
                key_query_lo(q, HG)

            def body(q):
                for g in range(HG):
                    for i in range(ST):
                        if g == 2 and not q.last and i < 2:
                            lo_tile(q, "xt", q.s + 1, i + 1, xt_h, xt_l, xt_hi)
                            if i == 0:
                                norm1(q, q.s + 1, q.s + 1, 3)
                        if unit_tile(g, i, q.last):
                            qk_tile(q, *unit_tile(g, i, q.last))
                        if g == 2 and not q.last and i == 1:
                            lo_tile(q, "xt", q.s + 1, 3, xt_h, xt_l, xt_hi)
                        if i == 0 and g:
                            out_scale(q, g - 1)
                        if i == 1 and (g < HG - 1 or not q.last):
                            key_query_lo(q, g + 1)
                        if g == 1 and i == 2 and not q.last:
                            stats1(q.s + 1, q.s + 1)
                    def first_tile():
                        lo_tile(q, "xt", q.s + 1, 0, xt_h, xt_l, xt_hi)
                        norm1(q, q.s + 1, q.s + 1, 2)

                    if g == 1 and not q.last:
                        norm1(q, q.s + 1, q.s + 1, 0)
                        norm1(q, q.s + 1, q.s + 1, 1)
                        lengths(q, g + 2, first_tile)
                    elif g < 2:
                        lengths(q, g + 2)
                    elif g == 2 and not q.last:
                        lengths(q, HG)
                out_scale(q, HG - 1)
                for what in tail:
                    t = int(what[1])
                    if what[0] == "q" and not q.last:
                        qk_tile(q, 1, 1, t)
                    if what[0] == "o":
                        residual(q, t)
                        stats2_of(q, t)
                        if t:
                            norm2(q, t - 1)
                    if what == "x1":
                        norm2(q, ST - 1)
                    if what[0] == "x":
                        lo_tile(q, "x2t", q.s, t, ot_h, ot_l, xt2_hi)
                V.tensor_scalar(q_const[:, bass.ds(q.s * ST, ST)], ve2[:], bqbk[:, 0:1], None, ALU.add)\
                    .then_inc(cb_done, 1)
                dve.wait_ge(cb_done, q.s + 1)
                if not q.last:
                    lengths(q, HG + 1)
                for m in range(DK):
                    dve.wait_ge(filled, q.filled(("qp", m)))
                    if m == 0:
                        dve.wait_ge(x1_stored, q.s * 16 + 16)
                    for t in range(ST):
                        last = V.tensor_scalar(xs_tile(q.s, t)[:, P * m:P * m + P],
                                               q.bank(("qp", m))[:, P * t:P * t + P],
                                               bqp[:, m:m + 1], None, ALU.add)
                    last.then_inc(released, 1)

            run(dve, lead_in, body)

        @block.tensor
        def _(pe):
            PE = nc.tensor

            def bank(q, key):
                pe.wait_ge(released, q.nth(key) + 1)
                return q.bank(key)

            def transposes(q, kind, n, t, done):
                out = bank(q, (kind, t))
                pe.wait_ge(done, n * ST + t + 1)
                for k in range(DK):
                    last = PE.transpose(out[:, P * k:P * k + P], xn[:, t % 2, P * k:P * k + P], ident[:])
                last.then_inc(filled, 1)

            def project_in(q, d, g, t):
                out = bank(q, ("qkv", d, g, t))
                if g == 0:
                    pe.wait_ge(released, q.read(("xt", t)))
                for k in range(DK):
                    last = three(PE, out[:, 0:GW], xt_h[:, k, P * t:P * t + P], xt_l[:, k, P * t:P * t + P],
                                 wqkv_h[:, k, g, :], wqkv_l[:, k, g, :], k == 0, k == DK - 1)
                last.then_inc(filled, 1)

            def head_transposes(q, g):
                pe.wait_ge(qk_done, q.group(g) + 1)
                for kind, off in (("kt", P), ("qt", 0)):
                    out = bank(q, (kind, g))
                    for t in range(ST):
                        last = PE.transpose(out[:, P * t:P * t + P], qk[:, g % 2, t, off:off + P], ident[:])
                    last.then_inc(filled, 1)

            def scores(q, n, first=False):
                g, i = n // ST, n % ST
                lo, w, c0 = window(i)
                unit = n - HG * ST if q.lead else q.group(0) * ST + n
                if i == 0:
                    pe.wait_ge(released, q.read(("qt", g)))
                if not first:
                    pe.wait_ge(exp_done, unit - 1)
                for a in range(2):
                    out = score[:, 2 * (n % 2) + a, 0:2 * WIN].rearrange("p (h w) -> p h w", h=2)[:, :, 0:w]
                    last = three(PE, out, kt_h[:, g % 2, P * i:P * i + P], kt_l[:, g % 2, P * i:P * i + P],
                                 qbd_h[:, g % 2, 2 * a:2 * a + 2, lo:lo + w],
                                 qbd_l[:, g % 2, 2 * a:2 * a + 2, lo:lo + w], True, True)
                last.then_inc(s_ready, 1)

            def weighted(q, n):
                g, i = n // ST, n % ST
                lo, w, c0 = window(i)
                pe.wait_ge(p_ready, q.group(0) * ST + n + 1)
                if i == 0 and g:
                    pe.wait_ge(o_copied, 2 * q.group(g))
                for h in range(HPG):
                    r = slice(DH * h, DH * h + DH)
                    PE.matmul(work[r, 2, lo:lo + w], v[:, g, i, DH * h:DH * h + DH],
                              probs[:, n % 2, h, 0:w], start=i == 0, stop=i == ST - 1,
                              skip_group_check=True)
                for h in range(HPG):
                    r = slice(DH * h, DH * h + DH)
                    last = PE.matmul(work[r, 3, lo:lo + w], ones[:], probs[:, n % 2, h, 0:w],
                                     start=i == 0, stop=i == ST - 1, skip_group_check=True)
                last.then_inc(pv_done, 1)

            def project_out(q, t):
                if t % 2 == 0:
                    pe.wait_ge(ot_lo, q.scaled(HG - 1) + t // 2 + 1)
                out = bank(q, ("op", t))
                for g in range(HG):
                    last = three(PE, out, ot_h[:, g, P * t:P * t + P], ot_l[:, g, P * t:P * t + P],
                                 wo_h[:, g, :], wo_l[:, g, :], g == 0, g == HG - 1)
                last.then_inc(filled, 1)

            def lead_in(q):
                for t in range(ST):
                    transposes(q, "xt", 0, t, xn_done)
                for g in range(2):
                    for t in range(ST):
                        project_in(q, 1, g, t)
                head_transposes(q, HG)
                scores(q, HG * ST, True)
                scores(q, HG * ST + 1, True)

            def body(q):
                for g in range(HG):
                    for i in range(ST):
                        n = ST * g + i
                        if g == 2 and not q.last and i < 2:
                            transposes(q, "xt", q.s + 1, i + 1, xn_done)
                        if unit_tile(g, i, q.last):
                            project_in(q, *unit_tile(g, i, q.last))
                        weighted(q, n)
                        if g == 2 and not q.last and i == 1:
                            transposes(q, "xt", q.s + 1, 3, xn_done)
                        if i == 1 and (g < HG - 1 or not q.last):
                            head_transposes(q, g + 1)
                        if n + 2 < HG * ST or not q.last:
                            scores(q, n + 2)
                        if g == 1 and not q.last and i == 3:
                            transposes(q, "xt", q.s + 1, 0, xn_done)
                for what in tail:
                    t = int(what[1])
                    if what[0] == "q" and not q.last:
                        project_in(q, 1, 1, t)
                    if what[0] == "o":
                        project_out(q, t)
                    if what[0] == "x":
                        transposes(q, "x2t", q.s, t, xn2_done)
                pe.wait_ge(released, q.read(("x2t", ST - 1)))
                for m in range(DK):
                    out = bank(q, ("qp", m))
                    for k in range(DK):
                        last = three(PE, out, wp_h[:, k, P * m:P * m + P], wp_l[:, k, P * m:P * m + P],
                                     ot_h[:, k, :], ot_l[:, k, :], k == 0, k == DK - 1)
                    last.then_inc(filled, 1)

            run(pe, lead_in, body)


def cross_phase(nc, scope, sb, sem, score, work, ident, q_const,
                ctx_n, wv, bv, x1_dram, qp_dram, x2_dram):
    cn_h = sb(scope, "cn_h", [P, CK, D], F32R)
    cn_l = sb(scope, "cn_l", [P, CK, D], F32R)
    ct_h = sb(scope, "ct_h", [P, DK, CTX], F32R)
    ct_l = sb(scope, "ct_l", [P, DK, CTX], F32R)
    wv_h = sb(scope, "wv_h", [P, DK, D], F32R)
    wv_l = sb(scope, "wv_l", [P, DK, D], F32R)
    bv_row = sb(scope, "bv_row", [P, D])
    stage = sb(scope, "x_stage", [P, 4, 2, D])
    q_raw = sb(scope, "x_q_raw", [P, D])
    q_h = sb(scope, "x_q_h", [P, 2, D], F32R)
    q_l = sb(scope, "x_q_l", [P, 2, D], F32R)
    pr = sb(scope, "x_pr", [P, CTX])
    pt_h = sb(scope, "pt_h", [P, CK, P], F32R)
    pt_l = sb(scope, "pt_l", [P, CK, P], F32R)
    o = sb(scope, "x_o", [P, D])
    ot_h = sb(scope, "x_ot_h", [P, D], F32R)
    ot_l = sb(scope, "x_ot_l", [P, D], F32R)
    xr = sb(scope, "xr", [P, 2, D])
    mx = sb(scope, "mx", [P, 4])
    negm = sb(scope, "negm", [P, 2])
    shift = sb(scope, "shift", [P, 2])
    sums = sb(scope, "sums", [P, 4])
    rinv = sb(scope, "rinv", [P, 2])

    SB = CTX // 512
    NP = CK // 2
    NW = DK // 2
    EARLY = 4
    staged = [sem(f"ctx_staged{i}") for i in range(4)]
    nat_hi = sem("nat_hi")
    nat_lo = sem("nat_lo")
    ct_ready = sem("ct_ready")
    ct_hi = sem("ct_hi_done")
    ct_lo = sem("ct_lo_done")
    bv_landed = sem("bv_landed")
    q_landed = sem("q_landed")
    q_hi = sem("xq_hi")
    q_lo = sem("xq_lo")
    sc_ready = sem("xs_ready")
    mx_done = sem("mx_done")
    m_done = sem("m_done")
    negm_done = sem("negm_done")
    shift_done = sem("shift_done")
    e_done = sem("e_done")
    sum_done = sem("sum_done")
    rinv_done = sem("rinv_done")
    pt_ready = sem("pt_ready")
    pth_done = sem("pth_done")
    ptl_done = sem("ptl_done")
    o_ready = sem("o_ready")
    o_done = sem("o_done")
    tr_ready = sem("tr_ready")
    oth_done = sem("oth_done")
    otl_done = sem("otl_done")
    y_ready = sem("y_ready")
    x2_done = sem("x2_done")
    xr_landed = [sem(f"xr_landed{i}") for i in range(2)]
    xb_done = sem("xbv_done")
    x2_stored = [sem(f"x2_stored{i}") for i in range(2)]

    cn_v = ctx_n.rearrange("b (t p) d -> b p t d", p=P)
    wv_v = wv.rearrange("(k p) n -> p k n", p=P)

    items = [(0, p) for p in range(NP)] + [("wv", p) for p in range(NW)]
    items += [(b, p) for b in range(1, NB) for p in range(NP)]

    def nth(b, p):
        return items.index((b, p))

    def split_dst(b, p):
        hi, lo = (wv_h, wv_l) if b == "wv" else (cn_h, cn_l)
        return hi[:, 2 * p:2 * p + 2, :], lo[:, 2 * p:2 * p + 2, :]

    def starts(g):
        return isinstance(g, int) and g == 0

    def tiles(eng, b, body):
        body(0, 0, 0)
        body(1, 1, 0)
        with eng.Fori(0, (BT - 4) // 2) as j:
            body(j * 2 + 2, 0, j + 1)
            body(j * 2 + 3, 1, j + 1)
        body(BT - 2, 0, BT // 2 - 1)
        body(BT - 1, 1, BT // 2 - 1)

    with nc.Block() as block:
        @block.sync
        def _(sp):
            def load_piece(b, p):
                n = nth(b, p)
                if n >= 4:
                    sp.wait_ge(nat_lo, n - 3)
                    b0, p0 = items[n - 4]
                    if b0 != "wv":
                        sp.wait_ge(ct_ready, b0 * CK + 2 * p0 + 2)
                src = wv_v if b == "wv" else cn_v[b]
                sp.dma_start(stage[:, n % 4], src[:, 2 * p:2 * p + 2, :]).then_inc(staged[n % 4], 16)

            def load_q(g):
                if not starts(g):
                    sp.wait_ge(q_lo, g)
                row = qp_dram[g] if isinstance(g, int) else qp_dram[bass.ds(g, 1)].rearrange("a p n -> (a p) n")
                sp.dma_start(q_raw[:], row).then_inc(q_landed, 16)

            load_piece(0, 0)
            load_q(0)
            load_piece(0, 1)
            load_piece(0, 2)
            load_q(1)
            for n in range(3, NP):
                load_piece(0, n)
            for p in range(NW):
                load_piece("wv", p)
            sp.dma_start(bv_row[:], bv.partition_broadcast(P)).then_inc(bv_landed, 16)
            for b in range(NB):
                if b + 1 < NB:
                    for p in range(EARLY):
                        load_piece(b + 1, p)

                def load(t, par, before):
                    g = b * BT + t
                    slot = b * (BT // 2) + before
                    if not starts(slot):
                        sp.wait_ge(x2_stored[par], slot * 16)
                    sp.dma_start(xr[:, par, :], x1_dram[bass.ds(g * P, P), :]).then_inc(xr_landed[par], 16)
                    if not isinstance(g, int) or g + 2 < NB * BT:
                        load_q(g + 2)
                    if isinstance(t, int) and t == BT - 1 and b + 1 < NB:
                        for p in range(EARLY, NP):
                            load_piece(b + 1, p)
                    if not starts(g):
                        sp.wait_ge(x2_done, g)
                        sp.dma_start(x2_dram[bass.ds((g - 1) * P, P), :], xr[:, 1 - par, :])\
                            .then_inc(x2_stored[1 - par], 16)

                tiles(sp, b, load)
            g = NB * BT
            sp.wait_ge(x2_done, g)
            sp.dma_start(x2_dram[(g - 1) * P:g * P, :], xr[:, 1, :]).then_inc(x2_stored[1], 16)
            for i in range(2):
                sp.wait_ge(x2_stored[i], NB * BT // 2 * 16)

        @block.gpsimd
        def _(pool):
            pool.wait_ge(bv_landed, 16)
            for b in range(NB):
                def body(t, par, before):
                    pool.wait_ge(xr_landed[par], (b * (BT // 2) + before) * 16 + 16)
                    nc.gpsimd.tensor_tensor(xr[:, par, :], xr[:, par, :], bv_row[:], ALU.add).then_inc(xb_done, 1)
                tiles(pool, b, body)

        @block.scalar
        def _(act):
            def q_high(g, par):
                act.wait_ge(q_landed, g * 16 + 16)
                nc.scalar.copy(q_h[:, par, :], q_raw[:]).then_inc(q_hi, 1)

            def natural(b, p):
                n = nth(b, p)
                act.wait_ge(staged[n % 4], 16 * (n // 4) + 16)
                nc.scalar.copy(split_dst(b, p)[0], stage[:, n % 4]).then_inc(nat_hi, 1)

            def turned(b, tile):
                act.wait_ge(ct_ready, b * CK + tile + 1)
                nc.scalar.copy(ct_h[:, :, P * tile:P * tile + P],
                               work[:, tile % 2, :].rearrange("p (k c) -> p k c", k=DK)).then_inc(ct_hi, 1)

            def exps(g, par):
                act.wait_ge(shift_done, g + 1)
                if not starts(g):
                    act.wait_ge(pt_ready, g * 4)
                    act.wait_ge(sum_done, g)
                for c in range(SB):
                    nc.scalar.activation(pr[:, 512 * c:512 * c + 512], score[:, c, :], ACT.Exp,
                                         bias=shift[:, par:par + 1], accum_out=sums[:, c:c + 1])\
                        .then_inc(e_done, 1)

            def finish(g):
                act.wait_ge(tr_ready, g + 1)
                nc.scalar.copy(ot_h[:], work[:, 3, :]).then_inc(oth_done, 1)

            for b in range(NB):
                g0 = b * BT
                if b == 0:
                    for p in range(NP):
                        turned(b, 2 * p)
                        turned(b, 2 * p + 1)
                        natural(b, p)
                        if p < 2:
                            q_high(p, p)
                else:
                    for p in range(EARLY):
                        natural(b, p)
                        if p == 1:
                            finish(g0 - 1)
                    for p in range(EARLY, NP):
                        turned(b, 2 * p)
                        turned(b, 2 * p + 1)
                        natural(b, p)
                exps(g0, 0)
                if b == 0:
                    for p in range(NW):
                        natural("wv", p)

                def body(t, par, before):
                    g = b * BT + t
                    head = isinstance(t, int) and t == 0
                    end = isinstance(t, int) and t == BT - 1
                    for c in range(4):
                        act.wait_ge(pt_ready, g * 4 + c + 1)
                        nc.scalar.copy(pt_h[:, 4 * c:4 * c + 4, :],
                                       work[:, c % 2, :].rearrange("p (k q) -> p k q", q=P)).then_inc(pth_done, 1)
                        if c == 1 and not head:
                            finish(g - 1)
                    if not end:
                        exps(g + 1, 1 - par)
                    if not isinstance(g, int) or g + 2 < NB * BT:
                        q_high(g + 2, par)
                    if end and b + 1 < NB:
                        for tile in range(2 * EARLY):
                            turned(b + 1, tile)
                    act.wait_ge(o_ready, g + 1)
                    act.wait_ge(rinv_done, g + 1)
                    nc.scalar.mul(o[:], work[:, 2, :], rinv[:, par:par + 1]).then_inc(o_done, 1)
                tiles(act, b, body)
            finish(NB * BT - 1)

        @block.vector
        def _(dve):
            V = nc.vector

            def q_low(g, par):
                dve.wait_ge(q_hi, g + 1)
                V.tensor_tensor(q_l[:, par, :], q_raw[:], q_h[:, par, :].bitcast(F32), ALU.subtract)\
                    .then_inc(q_lo, 1)

            def natural(b, p):
                n = nth(b, p)
                hi, lo = split_dst(b, p)
                dve.wait_ge(nat_hi, n + 1)
                V.tensor_tensor(lo, stage[:, n % 4], hi.bitcast(F32), ALU.subtract).then_inc(nat_lo, 1)

            def turned(b, tile):
                c = slice(P * tile, P * tile + P)
                dve.wait_ge(ct_hi, b * CK + tile + 1)
                V.tensor_tensor(ct_l[:, :, c], work[:, tile % 2, :].rearrange("p (k c) -> p k c", k=DK),
                                ct_h[:, :, c].bitcast(F32), ALU.subtract).then_inc(ct_lo, 1)

            def maxima(g, c):
                dve.wait_ge(sc_ready, g * SB + c + 1)
                V.reduce_max(mx[:, c:c + 1], score[:, c, :], AX.X).then_inc(mx_done, 1)

            def shifts(g, par):
                dve.wait_ge(mx_done, g * SB + SB)
                V.reduce_max(negm[:, par:par + 1], mx[:], AX.X).then_inc(m_done, 1)
                dve.wait_ge(m_done, g + 1)
                qc = q_const[:, bass.ds(g, 1)]
                V.tensor_scalar(negm[:, par:par + 1], negm[:, par:par + 1], qc, -1.0, ALU.add, ALU.mult)\
                    .then_inc(negm_done, 1)
                dve.wait_ge(negm_done, g + 1)
                V.tensor_tensor(shift[:, par:par + 1], negm[:, par:par + 1], qc, ALU.add)\
                    .then_inc(shift_done, 1)

            def total(g, par):
                dve.wait_ge(e_done, g * SB + SB)
                V.reduce_sum(rinv[:, par:par + 1], sums[:], AX.X).then_inc(sum_done, 1)
                dve.wait_ge(sum_done, g + 1)
                V.reciprocal(rinv[:, par:par + 1], rinv[:, par:par + 1]).then_inc(rinv_done, 1)

            def finish(g):
                dve.wait_ge(oth_done, g + 1)
                V.tensor_tensor(ot_l[:], work[:, 3, :], ot_h[:].bitcast(F32), ALU.subtract).then_inc(otl_done, 1)

            def result(g, par):
                dve.wait_ge(y_ready, g + 1)
                dve.wait_ge(xb_done, g + 1)
                V.tensor_tensor(xr[:, par, :], work[:, 3, :], xr[:, par, :], ALU.add).then_inc(x2_done, 1)

            for b in range(NB):
                g0 = b * BT
                if b == 0:
                    for p in range(NP):
                        turned(b, 2 * p)
                        turned(b, 2 * p + 1)
                        natural(b, p)
                        if p < 2:
                            q_low(p, p)
                        if p % 2 and p > 1:
                            maxima(g0, p // 2 - 1)
                else:
                    for p in range(EARLY):
                        natural(b, p)
                        if p == 1:
                            finish(g0 - 1)
                    maxima(g0, 0)
                    maxima(g0, 1)
                    result(g0 - 1, 1)
                    for p in range(EARLY, NP):
                        turned(b, 2 * p)
                        turned(b, 2 * p + 1)
                        natural(b, p)
                    maxima(g0, 2)
                maxima(g0, 3)
                shifts(g0, 0)
                total(g0, 0)
                if b == 0:
                    for p in range(NW):
                        natural("wv", p)

                def body(t, par, before):
                    g = b * BT + t
                    head = isinstance(t, int) and t == 0
                    end = isinstance(t, int) and t == BT - 1
                    for c in range(4):
                        dve.wait_ge(pth_done, g * 4 + c + 1)
                        V.tensor_tensor(pt_l[:, 4 * c:4 * c + 4, :],
                                        work[:, c % 2, :].rearrange("p (k q) -> p k q", q=P),
                                        pt_h[:, 4 * c:4 * c + 4, :].bitcast(F32), ALU.subtract)\
                            .then_inc(ptl_done, 1)
                        if not end:
                            maxima(g + 1, c)
                        if c == 1 and not head:
                            finish(g - 1)
                        if c == 2 and not head:
                            result(g - 1, 1 - par)
                    if not end:
                        shifts(g + 1, 1 - par)
                        total(g + 1, 1 - par)
                    if not isinstance(g, int) or g + 2 < NB * BT:
                        q_low(g + 2, par)
                    if end and b + 1 < NB:
                        for tile in range(2 * EARLY):
                            turned(b + 1, tile)
                tiles(dve, b, body)
            finish(NB * BT - 1)
            result(NB * BT - 1, 1)

        @block.tensor
        def _(pe):
            PE = nc.tensor

            def turn_context(b, tile):
                n = nth(b, tile // 2)
                pe.wait_ge(staged[n % 4], 16 * (n // 4) + 16)
                if tile >= 2:
                    pe.wait_ge(ct_lo, b * CK + tile - 1)
                elif b:
                    pe.wait_ge(ptl_done, b * BT * 4)
                for k in range(DK):
                    last = PE.transpose(work[:, tile % 2, P * k:P * k + P],
                                        stage[:, n % 4, tile % 2, P * k:P * k + P], ident[:])
                last.then_inc(ct_ready, 1)

            def scores(b, g, par, c, head):
                if c == 0:
                    pe.wait_ge(q_lo, g + 1)
                if head:
                    pe.wait_ge(ct_lo, b * CK + 4 * c + 4)
                if not starts(g):
                    pe.wait_ge(e_done, (g - 1) * SB + SB)
                for k in range(DK):
                    last = three(PE, score[:, c, :], q_h[:, par, P * k:P * k + P], q_l[:, par, P * k:P * k + P],
                                 ct_h[:, k, 512 * c:512 * c + 512], ct_l[:, k, 512 * c:512 * c + 512],
                                 k == 0, k == DK - 1)
                last.then_inc(sc_ready, 1)

            def transposes(b, g, c, head):
                pe.wait_ge(e_done, g * SB + c + 1)
                if c >= 2:
                    pe.wait_ge(ptl_done, g * 4 + c - 1)
                elif head:
                    pe.wait_ge(ct_lo, b * CK + CK)
                else:
                    pe.wait_ge(ptl_done, (g - 1) * 4 + c + 3)
                for k in range(4):
                    last = PE.transpose(work[:, c % 2, P * k:P * k + P],
                                        pr[:, 512 * c + P * k:512 * c + P * k + P], ident[:])
                last.then_inc(pt_ready, 1)

            def turn(g):
                pe.wait_ge(o_done, g + 1)
                if not starts(g):
                    pe.wait_ge(x2_done, g)
                for k in range(DK):
                    last = PE.transpose(work[:, 3, P * k:P * k + P], o[:, P * k:P * k + P], ident[:])
                last.then_inc(tr_ready, 1)

            def project(g):
                pe.wait_ge(otl_done, g + 1)
                for k in range(DK):
                    last = three(PE, work[:, 3, :], ot_h[:, P * k:P * k + P], ot_l[:, P * k:P * k + P],
                                 wv_h[:, k, :], wv_l[:, k, :], k == 0, k == DK - 1)
                last.then_inc(y_ready, 1)

            for b in range(NB):
                g0 = b * BT
                for c in range(SB):
                    for tile in range(4 * c, 4 * c + 4):
                        if b == 0 or tile >= 2 * EARLY:
                            turn_context(b, tile)
                    scores(b, g0, 0, c, True)
                    if b and c == 0:
                        turn(g0 - 1)
                    if b and c == 1:
                        project(g0 - 1)

                def body(t, par, before):
                    g = b * BT + t
                    head = isinstance(t, int) and t == 0
                    end = isinstance(t, int) and t == BT - 1
                    for c in range(4):
                        if not end:
                            scores(b, g + 1, 1 - par, c, False)
                        transposes(b, g, c, head)
                        if c == 1 and not head:
                            turn(g - 1)
                        if c == 2 and not head:
                            project(g - 1)
                    if head:
                        pe.wait_ge(nat_lo, nth(b, NP - 1) + 1)
                        if b == 0:
                            pe.wait_ge(nat_lo, nth("wv", NW - 1) + 1)
                    if not starts(g):
                        pe.wait_ge(o_done, g)
                    for kt in range(CK):
                        if kt % 4 == 0:
                            pe.wait_ge(ptl_done, g * 4 + kt // 4 + 1)
                        last_mm = three(PE, work[:, 2, :], pt_h[:, kt, :], pt_l[:, kt, :],
                                        cn_h[:, kt, :], cn_l[:, kt, :], kt == 0, kt == CK - 1)
                        if end and b + 1 < NB and kt % 2 == 0:
                            turn_context(b + 1, kt // 2)
                    last_mm.then_inc(o_ready, 1)
                tiles(pe, b, body)
            turn(NB * BT - 1)
            project(NB * BT - 1)


def ffn_phase(nc, scope, sb, sem, score, work, ident, mhalf, wait_pad, wg_t, wu_t, wd_t, x2_dram, out):
    wg_h = sb(scope, "wg_h", [P, DK, FH], F32R)
    wg_l = sb(scope, "wg_l", [P, DK, FH], F32R)
    wu_h = sb(scope, "wu_h", [P, DK, FH], F32R)
    wu_l = sb(scope, "wu_l", [P, DK, FH], F32R)
    wd_h = sb(scope, "wd_h", [P, FK, D], F32R)
    wd_l = sb(scope, "wd_l", [P, FK, D], F32R)
    stage = sb(scope, "w_stage", [P, 2, 3, 512], I32)
    xs = sb(scope, "fx", [P, 2, ST, D])
    xn = sb(scope, "fxn", [P, 2, D])
    xt_h = sb(scope, "fxt_h", [P, DK, SEQ], F32R)
    xt_l = sb(scope, "fxt_l", [P, DK, SEQ], F32R)
    gate = sb(scope, "gate", [P, 2, SEQ])
    hid = sb(scope, "hid", [P, SEQ])
    hid_h = sb(scope, "hid_h", [P, 2, SEQ], F32R)
    hid_l = sb(scope, "hid_l", [P, 2, SEQ], F32R)
    stats = sb(scope, "fstats", [P, ST, 6])
    mv = sb(scope, "fmv", [P, ST, 2])
    ve = sb(scope, "fve", [P, ST])
    rstd = sb(scope, "frstd", [P, ST])

    w_staged = [[sem(f"w_staged{i}{j}") for j in range(3)] for i in range(2)]
    w_hi = sem("fw_hi")
    w_lo = sem("fw_lo")
    x_landed = sem("fx_landed")
    st_done = sem("fst_done")
    ag_done = sem("fag_done")
    ve_done = sem("fve_done")
    rstd_done = sem("frstd_done")
    xn_done = sem("fxn_done")
    xt_ready = sem("fxt_ready")
    xt_hi = sem("fxt_hi_done")
    xt_lo = sem("fxt_lo_done")
    gu_ready = sem("gu_ready")
    gate_done = sem("gate_done")
    hid_done = sem("hid_done")
    hidh_done = sem("hidh_done")
    hidl_done = sem("hidl_done")
    down_done = sem("down_done")
    y_done = sem("fy_done")
    stored = sem("fstored")

    x_v = x2_dram.rearrange("(s t p) d -> s p t d", t=ST, p=P)
    o_v = out.rearrange("(s t p) d -> s p t d", t=ST, p=P)
    wg_v = wg_t.rearrange("(k p) n -> p k n", p=P)
    wu_v = wu_t.rearrange("(k p) n -> p k n", p=P)
    wd_v = wd_t.rearrange("(f p) n -> p f n", p=P)

    def parts(f):
        c = slice(P * f, P * f + P)
        return (wg_h[:, :, c], wg_l[:, :, c]), (wu_h[:, :, c], wu_l[:, :, c]), (wd_h[:, f, :], wd_l[:, f, :])

    def staged_view(f, j):
        raw = stage[:, f % 2, j, :]
        return raw if j == 2 else raw.rearrange("p (k c) -> p k c", k=DK)

    def x_tile(s, t):
        if isinstance(s, int):
            return xs[:, s % 2, t, :]
        return xs[:].rearrange("p a t d -> p (a t) d")[:, bass.ds((s % 2) * ST + t, 1), :]\
            .rearrange("p a d -> p (a d)")

    def run(eng, body):
        body(eng, 0, True, False)
        with eng.Fori(1, NBLK - 1) as s:
            body(eng, s, False, False)
        body(eng, NBLK - 1, False, True)

    with nc.Block() as block:
        @block.sync
        def _(sp):
            sp.dma_start(xs[:, 0], x_v[0]).then_inc(x_landed, 16)
            for f in range(FK):
                if f >= 2:
                    sp.wait_ge(w_lo, 3 * (f - 1))
                srcs = (wg_v[:, :, P * f:P * f + P], wu_v[:, :, P * f:P * f + P], wd_v[:, f, :])
                for j in range(3):
                    sp.dma_start(staged_view(f, j), srcs[j]).then_inc(w_staged[f % 2][j], 16)
            sp.wait_ge(x_landed, 16)
            sp.dma_start(xs[:, 1], x_v[1]).then_inc(x_landed, 16)
            for s in range(NBLK):
                sp.wait_ge(y_done, s * ST + ST)
                sp.dma_start(o_v[s], xs[:, s % 2]).then_inc(stored, 16)
                if s + 2 < NBLK:
                    sp.wait_ge(stored, s * 16 + 16)
                    sp.wait_ge(x_landed, s * 16 + 32)
                    sp.dma_start(xs[:, s % 2], x_v[s + 2]).then_inc(x_landed, 16)
            sp.wait_ge(stored, NBLK * 16)

        @block.gpsimd
        def _(pool):
            with pool.Fori(0, NBLK) as s:
                pool.wait_ge(ve_done, s + 1)
                nc.gpsimd.tensor_tensor(rstd[:], ve[:], mhalf[:, 0:ST], ALU.pow).then_inc(rstd_done, 1)

        def act_block(act, s, load, last):
            def turned(s, t):
                act.wait_ge(xt_ready, s * ST + t + 1)
                nc.scalar.copy(xt_h[:, :, P * t:P * t + P],
                               score[:, t % 2, :].rearrange("p (k c) -> p k c", k=DK)).then_inc(xt_hi, 1)

            def weights_hi(f):
                for j in range(3):
                    act.wait_ge(w_staged[f % 2][j], 16 * (f // 2) + 16)
                    nc.scalar.copy(parts(f)[j][0], staged_view(f, j)).then_inc(w_hi, 1)

            if load:
                weights_hi(0)
                weights_hi(1)
                for t in range(ST):
                    turned(0, t)
            for f in range(FK):
                act.wait_ge(gu_ready, s * FK + f + 1)
                if f >= 2:
                    act.wait_ge(hid_done, s * FK + f - 1)
                nc.scalar.activation(gate[:, f % 2, :], score[:, 2 * (f % 2), :], ACT.Silu, scale=WSCALE)\
                    .then_inc(gate_done, 1)
                if f == FK - 1 and not last:
                    turned(s + 1, 0)
                act.wait_ge(hid_done, s * FK + f + 1)
                if f >= 2:
                    act.wait_ge(down_done, s * FK + f - 1)
                nc.scalar.copy(hid_h[:, f % 2, :], hid[:]).then_inc(hidh_done, 1)
                if load and f + 2 < FK:
                    weights_hi(f + 2)
            if not last:
                for t in range(1, ST):
                    turned(s + 1, t)

        @block.scalar
        def _(act):
            run(act, act_block)

        def dve_block(dve, s, load, last):
            V = nc.vector

            def weights_lo(f):
                for j in range(3):
                    hi, lo = parts(f)[j]
                    dve.wait_ge(w_hi, 3 * f + j + 1)
                    V.tensor_tensor(lo, staged_view(f, j), hi.bitcast(F32), ALU.subtract).then_inc(w_lo, 1)

            def block_stats(s):
                dve.wait_ge(x_landed, s * 16 + 16)
                V.memset(wait_pad[:, 1:2], 0.0)
                for t in range(ST):
                    V.bn_stats(stats[:, t, :], x_tile(s, t)).then_inc(st_done, 1)
                dve.wait_ge(st_done, s * ST + ST)
                V.memset(wait_pad[:, 0:1], 0.0)
                for t in range(ST):
                    V.bn_aggr(mv[:, t, :], stats[:, t, :]).then_inc(ag_done, 1)
                dve.wait_ge(ag_done, s * ST + ST)
                V.tensor_scalar(ve[:], mv[:, :, 1], LN_EPS, None, ALU.add).then_inc(ve_done, 1)

            def norm(s, t):
                if t == 0:
                    dve.wait_ge(rstd_done, s + 1)
                if t >= 2:
                    dve.wait_ge(xt_ready, s * ST + t - 1)
                V.tensor_scalar(xn[:, t % 2, :], x_tile(s, t), mv[:, t, 0:1], rstd[:, t:t + 1],
                                ALU.subtract, ALU.mult).then_inc(xn_done, 1)

            def turned(s, t):
                dve.wait_ge(xt_hi, s * ST + t + 1)
                V.tensor_tensor(xt_l[:, :, P * t:P * t + P],
                                score[:, t % 2, :].rearrange("p (k c) -> p k c", k=DK),
                                xt_h[:, :, P * t:P * t + P].bitcast(F32), ALU.subtract).then_inc(xt_lo, 1)

            if load:
                block_stats(0)
                weights_lo(0)
                norm(0, 0)
                norm(0, 1)
                for t in range(ST):
                    if t + 2 < ST:
                        norm(0, t + 2)
                    turned(0, t)
                    if t == 0:
                        weights_lo(1)
            for f in range(FK):
                dve.wait_ge(gate_done, s * FK + f + 1)
                if f >= 1:
                    dve.wait_ge(hidl_done, s * FK + f)
                V.scalar_tensor_tensor(hid[:], score[:, 2 * (f % 2) + 1, :], WSCALE, gate[:, f % 2, :],
                                       ALU.mult, ALU.mult).then_inc(hid_done, 1)
                if f == FK - 1 and not last:
                    turned(s + 1, 0)
                dve.wait_ge(hidh_done, s * FK + f + 1)
                V.tensor_tensor(hid_l[:, f % 2, :], hid[:], hid_h[:, f % 2, :].bitcast(F32), ALU.subtract)\
                    .then_inc(hidl_done, 1)
                if load and f + 2 < FK:
                    weights_lo(f + 2)
                if f == FK - 4 and not last:
                    block_stats(s + 1)
                if f == FK - 3 and not last:
                    norm(s + 1, 0)
                    norm(s + 1, 1)
            if not last:
                norm(s + 1, 2)
                turned(s + 1, 1)
                norm(s + 1, 3)
                turned(s + 1, 2)
                turned(s + 1, 3)
            for t in range(ST):
                dve.wait_ge(down_done, s * FK + FK)
                V.scalar_tensor_tensor(x_tile(s, t), work[:, t, :], WSCALE, x_tile(s, t), ALU.mult, ALU.add)\
                    .then_inc(y_done, 1)

        @block.vector
        def _(dve):
            run(dve, dve_block)

        def pe_block(pe, s, load, last_block):
            PE = nc.tensor

            def turn(s, t):
                pe.wait_ge(xn_done, s * ST + t + 1)
                if t >= 2:
                    pe.wait_ge(xt_lo, s * ST + t - 1)
                elif not (isinstance(s, int) and s == 0):
                    pe.wait_ge(hid_done, s * FK - 1)
                for k in range(DK):
                    last = PE.transpose(score[:, t % 2, P * k:P * k + P], xn[:, t % 2, P * k:P * k + P], ident[:])
                last.then_inc(xt_ready, 1)

            def up(f):
                if load:
                    pe.wait_ge(w_lo, 3 * f + 3)
                if f == 0:
                    pe.wait_ge(xt_lo, s * ST + ST)
                if f >= 2:
                    pe.wait_ge(hid_done, s * FK + f - 1)
                elif f == 1 and not load:
                    pe.wait_ge(hid_done, s * FK)
                (g_h, g_l), (u_h, u_l), _ = parts(f)
                for bank, (w_h, w_l) in enumerate(((g_h, g_l), (u_h, u_l))):
                    for k in range(DK):
                        last = three(PE, score[:, 2 * (f % 2) + bank, :], w_h[:, k, :], w_l[:, k, :],
                                     xt_h[:, k, :], xt_l[:, k, :], k == 0, k == DK - 1)
                last.then_inc(gu_ready, 1)

            def down(f):
                pe.wait_ge(hidl_done, s * FK + f + 1)
                if f == 0 and not load:
                    pe.wait_ge(y_done, s * ST)
                for t in range(ST):
                    last = three(PE, work[:, t, :], hid_h[:, f % 2, P * t:P * t + P],
                                 hid_l[:, f % 2, P * t:P * t + P], wd_h[:, f, :], wd_l[:, f, :],
                                 f == 0, f == FK - 1)
                last.then_inc(down_done, 1)
                return last

            if load:
                for t in range(ST):
                    turn(0, t)
            up(0)
            for f in range(1, FK):
                up(f)
                if f == FK - 1 and not last_block:
                    turn(s + 1, 0)
                    turn(s + 1, 1)
                down(f - 1)
            if not last_block:
                turn(s + 1, 2)
                turn(s + 1, 3)
            down(FK - 1)

        @block.tensor
        def _(pe):
            run(pe, pe_block)


_OUT_SHAPE = (2, 1024, 512)


def kernel(**inputs):
    import numpy as np
    import concourse.bacc as bacc
    from concourse.bass_utils import run_bass_kernel_spmd

    def arr(name):
        return np.asarray(inputs[name])

    x = arr("x").reshape(2, 512, 2, 512).transpose(0, 2, 1, 3).reshape(2048, 512)
    laid = {
        "x": x,
        "ctx_n": arr("ctx_1024"),
        "wqkv_t": arr("L0_attn_qkv_w").T.reshape(512, 3, 4, 128).transpose(0, 2, 1, 3).reshape(512, 1536),
        "qkv_b": arr("L0_attn_qkv_b").reshape(3, 4, 128).transpose(1, 0, 2).reshape(1536),
        "wo_t": arr("L0_attn_out_w").T,
        "out_b": arr("L0_attn_out_b"),
        "wq_t": arr("L0_xattn_Wq").T,
        "bq": arr("L0_xattn_bq"),
        "wk_t": arr("L0_xattn_Wk").T,
        "bk": arr("L0_xattn_bk"),
        "wv": arr("L0_xattn_Wv"),
        "bv": arr("L0_xattn_bv"),
        "wg_t": arr("L0_ffn_w_gate").T,
        "wu_t": arr("L0_ffn_w_up").T,
        "wd_t": arr("L0_ffn_w_down").T,
    }
    nc = bacc.Bacc("TRN2", target_bir_lowering=False, num_devices=1)
    arrays, args = {}, []
    for name, a in laid.items():
        a = np.ascontiguousarray(a)
        arrays[f"in_{name}"] = a
        args.append(nc.dram_tensor(f"in_{name}", a.shape, mybir.dt.from_np(a.dtype), kind="ExternalInput").ap())
    args.append(nc.dram_tensor("out_y", (2048, 512), F32, kind="ExternalOutput").ap())
    decoder_layer(nc, *args)
    r = run_bass_kernel_spmd(nc, [arrays], core_ids=[0])
    y = r.results[0]["out_y"].reshape(2, 2, 512, 512).transpose(0, 2, 1, 3).reshape(_OUT_SHAPE)
    return np.ascontiguousarray(y)
```
